# Optimizing a Trainium2 kernel written in Bass

```python
import numpy as np
import jax
import jax.numpy as jnp

def _softmax(x, axis=-1):
    return jax.nn.softmax(x, axis=axis)
def _gelu(x):
    return jax.nn.gelu(x, approximate=True)
def _silu(x):
    return jax.nn.silu(x)
def _sigmoid(x):
    return jax.nn.sigmoid(x)
def _layernorm(x, axis=-1, eps=1e-5):
    m = jnp.mean(x, axis=axis, keepdims=True)
    v = jnp.var(x, axis=axis, keepdims=True)
    return (x - m) / jnp.sqrt(v + eps)
def _scatter_add(tgt, idx, src, axis=0):
    return tgt.at[idx].add(src)
def _segment_sum(src, seg, n):
    return jax.ops.segment_sum(src, seg, n)

kernel_name = 'mk_conv_preact_d2_conv_nhwc64_a54066'

def setup_inputs(seed: int = 0):
    np.random.seed(seed)
    _w = jnp.asarray
    def _rec_inputs():
        import jax
        import jax.numpy as jnp
        _gk = jax.random.key(seed)
        x = -0.000125 + 0.9999 * jax.random.normal(jax.random.fold_in(_gk, 1), (8, 256, 256, 64), jnp.float32)
        return x
    x = _rec_inputs()
    def _L0_conv_setup():
        import jax, jax.numpy as jnp
        import numpy as np
        WIN = 8
        HEADS = 4

        def _local_mixer(x1, w_qkv, b_qkv, pos_emb):
            b, h, w, half = x1.shape
            hb, wb = (h // WIN, w // WIN)
            hc = half // HEADS
            xw = x1.reshape(b, hb, WIN, wb, WIN, half).transpose(0, 1, 3, 2, 4, 5)
            xw = xw.reshape(b * hb * wb, WIN * WIN, half)
            qkv = jnp.einsum('bnc,dc->bnd', xw, w_qkv) + b_qkv
            q, k, v = jnp.split(qkv, 3, axis=-1)

            def heads(t):
                B, n, _ = t.shape
                return t.reshape(B, n, HEADS, hc).transpose(0, 2, 1, 3)
            q, k, v = (heads(q), heads(k), heads(v))
            q = q * hc ** (-0.5)
            sim = jnp.einsum('bhic,bhjc->bhij', q, k) + pos_emb
            attn = jax.nn.softmax(sim, axis=-1)
            out = jnp.einsum('bhij,bhjc->bhic', attn, v)
            out = out.transpose(0, 2, 1, 3).reshape(b * hb * wb, WIN * WIN, half)
            out = out.reshape(b, hb, wb, WIN, WIN, half).transpose(0, 1, 3, 2, 4, 5)
            return out.reshape(b, h, w, half)

        def _global_mixer(x2, amp_w, amp_b, pha_w, pha_b):
            b, h, w, half = x2.shape
            xc = x2.transpose(0, 3, 1, 2)
            fre = jnp.fft.rfft2(xc, axes=(-2, -1), norm='backward')
            amp = jnp.abs(fre)
            pha = jnp.angle(fre)
            cw = lambda p: p[None, :, None, None]
            amp_fea = amp * cw(amp_w) + cw(amp_b)
            pha_fea = pha * cw(pha_w) + cw(pha_b)
            real = amp_fea * jnp.cos(pha_fea) + 1e-08
            imag = amp_fea * jnp.sin(pha_fea) + 1e-08
            out = jax.lax.complex(real, imag) + 1e-08
            out = jnp.abs(jnp.fft.irfft2(out, s=(h, w), axes=(-2, -1), norm='backward'))
            return out.transpose(0, 2, 3, 1)
        key = jax.random.key(seed)
        ks = jax.random.split(key, 10)
        b, h, w, c = (8, 256, 256, 64)
        half = c // 2
        seq = WIN * WIN
        return {'x': jax.random.normal(ks[0], (b, h, w, c), jnp.float32), 'w_qkv': jax.random.normal(ks[1], (3 * half, half), jnp.float32) * 0.05, 'b_qkv': jax.random.normal(ks[2], (3 * half,), jnp.float32) * 0.02, 'pos_emb': jax.random.truncated_normal(ks[3], -2.0, 2.0, (1, HEADS, seq, seq), jnp.float32), 'amp_w': jax.random.normal(ks[4], (half,), jnp.float32) * 0.05 + 1.0, 'amp_b': jax.random.normal(ks[5], (half,), jnp.float32) * 0.02, 'pha_w': jax.random.normal(ks[6], (half,), jnp.float32) * 0.05 + 1.0, 'pha_b': jax.random.normal(ks[7], (half,), jnp.float32) * 0.02, 'proj_w': jax.random.normal(ks[8], (c, c), jnp.float32) * 0.05, 'proj_b': jax.random.normal(ks[9], (c,), jnp.float32) * 0.02}
    _L0_conv_all = _L0_conv_setup()
    _L0_conv_in = {k: v for k, v in _L0_conv_all.items() if k in ('w_qkv', 'b_qkv', 'pos_emb', 'amp_w', 'amp_b', 'pha_w', 'pha_b', 'proj_w', 'proj_b', )}
    del _L0_conv_all

    def _L1_conv_setup():
        import jax, jax.numpy as jnp
        import numpy as np
        key = jax.random.key(seed)
        k1, k2 = jax.random.split(key)
        B, H, W, C, K = (16, 128, 256, 64, 5)
        inputs = jax.random.normal(k1, (B, H, W, C), dtype=jnp.float32)
        w = jax.random.uniform(k2, (C, K, 1, C), dtype=jnp.float32, minval=-0.05, maxval=0.05)
        b = jnp.zeros((C,), dtype=jnp.float32)
        return {'inputs': inputs, 'w': w, 'b': b}
    _L1_conv_all = _L1_conv_setup()
    _L1_conv_in = {k: v for k, v in _L1_conv_all.items() if k in ('w', 'b', )}
    del _L1_conv_all

    return {
        "x": x,
        "L0_conv_w_qkv": _L0_conv_in["w_qkv"],
        "L0_conv_b_qkv": _L0_conv_in["b_qkv"],
        "L0_conv_pos_emb": _L0_conv_in["pos_emb"],
        "L0_conv_amp_w": _L0_conv_in["amp_w"],
        "L0_conv_amp_b": _L0_conv_in["amp_b"],
        "L0_conv_pha_w": _L0_conv_in["pha_w"],
        "L0_conv_pha_b": _L0_conv_in["pha_b"],
        "L0_conv_proj_w": _L0_conv_in["proj_w"],
        "L0_conv_proj_b": _L0_conv_in["proj_b"],
        "L1_conv_w": _L1_conv_in["w"],
        "L1_conv_b": _L1_conv_in["b"],
    }

def reference(x, L0_conv_w_qkv, L0_conv_b_qkv, L0_conv_pos_emb, L0_conv_amp_w, L0_conv_amp_b, L0_conv_pha_w, L0_conv_pha_b, L0_conv_proj_w, L0_conv_proj_b, L1_conv_w, L1_conv_b):
    import jax
    import jax.numpy as jnp
    def _L0_conv_ref(x, w_qkv, b_qkv, pos_emb, amp_w, amp_b, pha_w, pha_b, proj_w, proj_b):
        import jax, jax.numpy as jnp
        import numpy as np
        WIN = 8
        HEADS = 4

        def _local_mixer(x1, w_qkv, b_qkv, pos_emb):
            b, h, w, half = x1.shape
            hb, wb = (h // WIN, w // WIN)
            hc = half // HEADS
            xw = x1.reshape(b, hb, WIN, wb, WIN, half).transpose(0, 1, 3, 2, 4, 5)
            xw = xw.reshape(b * hb * wb, WIN * WIN, half)
            qkv = jnp.einsum('bnc,dc->bnd', xw, w_qkv) + b_qkv
            q, k, v = jnp.split(qkv, 3, axis=-1)

            def heads(t):
                B, n, _ = t.shape
                return t.reshape(B, n, HEADS, hc).transpose(0, 2, 1, 3)
            q, k, v = (heads(q), heads(k), heads(v))
            q = q * hc ** (-0.5)
            sim = jnp.einsum('bhic,bhjc->bhij', q, k) + pos_emb
            attn = jax.nn.softmax(sim, axis=-1)
            out = jnp.einsum('bhij,bhjc->bhic', attn, v)
            out = out.transpose(0, 2, 1, 3).reshape(b * hb * wb, WIN * WIN, half)
            out = out.reshape(b, hb, wb, WIN, WIN, half).transpose(0, 1, 3, 2, 4, 5)
            return out.reshape(b, h, w, half)

        def _global_mixer(x2, amp_w, amp_b, pha_w, pha_b):
            b, h, w, half = x2.shape
            xc = x2.transpose(0, 3, 1, 2)
            fre = jnp.fft.rfft2(xc, axes=(-2, -1), norm='backward')
            amp = jnp.abs(fre)
            pha = jnp.angle(fre)
            cw = lambda p: p[None, :, None, None]
            amp_fea = amp * cw(amp_w) + cw(amp_b)
            pha_fea = pha * cw(pha_w) + cw(pha_b)
            real = amp_fea * jnp.cos(pha_fea) + 1e-08
            imag = amp_fea * jnp.sin(pha_fea) + 1e-08
            out = jax.lax.complex(real, imag) + 1e-08
            out = jnp.abs(jnp.fft.irfft2(out, s=(h, w), axes=(-2, -1), norm='backward'))
            return out.transpose(0, 2, 3, 1)
        b, h, w, c = x.shape
        half = c // 2
        x1 = _local_mixer(x[..., :half], w_qkv, b_qkv, pos_emb)
        x2 = _global_mixer(x[..., half:], amp_w, amp_b, pha_w, pha_b)
        cat = jnp.concatenate([x1, x2], axis=-1)
        out = jnp.einsum('bhwc,dc->bhwd', cat, proj_w) + proj_b
        return out

    def _L1_conv_ref(inputs, w, b):
        import jax, jax.numpy as jnp
        import numpy as np
        B, H, W, C = inputs.shape
        K = w.shape[1]
        pad_l = (K - 1) // 2
        pad_r = K - 1 - pad_l
        kernel = jnp.transpose(w[:, :, 0, :], (1, 0, 2))

        def conv_col(col):
            return jax.lax.conv_general_dilated(col, kernel, window_strides=(1,), padding=[(pad_l, pad_r)], dimension_numbers=('NWC', 'WIO', 'NWC'))

        def step(h, xcol):
            g = jax.nn.relu(conv_col(xcol + h) + b)
            return (g, g)
        xs = jnp.moveaxis(inputs, 2, 0)[::-1]
        h0 = jnp.zeros((B, H, C), dtype=inputs.dtype)
        _, gs = jax.lax.scan(step, h0, xs)
        return jnp.moveaxis(gs[::-1], 0, 2)

    def _gn(v, G=32, eps=1e-5):
        B_, H_, W_, C_ = v.shape
        g = v.reshape(B_, H_, W_, G, C_ // G)
        m = jnp.mean(g, axis=(1, 2, 4), keepdims=True)
        s = jnp.var(g, axis=(1, 2, 4), keepdims=True)
        return ((g - m) / jnp.sqrt(s + eps)).reshape(v.shape)

    def _ln_c(v, eps=1e-6):
        m = jnp.mean(v, axis=-1, keepdims=True)
        s = jnp.var(v, axis=-1, keepdims=True)
        return (v - m) / jnp.sqrt(s + eps)

    def _ln_t(v, eps=1e-5):
        m = jnp.mean(v, axis=-1, keepdims=True)
        s = jnp.var(v, axis=-1, keepdims=True)
        return (v - m) / jnp.sqrt(s + eps)

    def _to_tokens(v):
        B_, H_, W_, C_ = v.shape
        return v.reshape(B_, H_ * W_, C_)
    def _from_tokens(t, like):
        return t.reshape(like.shape)

    x = x + _L0_conv_ref(_gn(x), L0_conv_w_qkv, L0_conv_b_qkv, L0_conv_pos_emb, L0_conv_amp_w, L0_conv_amp_b, L0_conv_pha_w, L0_conv_pha_b, L0_conv_proj_w, L0_conv_proj_b)
    x = x + _L1_conv_ref(_gn(x), L1_conv_w, L1_conv_b)
    return x


_drawn_inputs = setup_inputs


def setup_inputs(seed=0):
    import zlib

    import numpy as np

    out = dict(_drawn_inputs(seed))
    spreads = {'L1_conv_b': (0.0, 0.1)}
    factors = {'L0_conv_w_qkv': 4.38,
     'L0_conv_b_qkv': 8.0,
     'L0_conv_pos_emb': 6.467,
     'L0_conv_amp_w': 4.758,
     'L0_conv_amp_b': 8.0,
     'L0_conv_pha_b': 8.0,
     'L0_conv_proj_b': 2.816}
    for name, (base, spread) in spreads.items():
        noise = np.random.default_rng([zlib.crc32(name.encode()), seed]).standard_normal(out[name].shape)
        drawn = base * np.exp(spread * noise) if base else spread * noise
        out[name] = jnp.asarray(drawn.astype(out[name].dtype))
    for name, factor in factors.items():
        out[name] = (out[name] * factor).astype(out[name].dtype)
    return out
```

```python
import numpy as np
import concourse.bass as bass
from concourse import mybir
from contextlib import ExitStack

F32 = mybir.dt.float32
ALU = mybir.AluOpType
ACT = mybir.ActivationFunctionType
AX = mybir.AxisListType
H, W, C = 256, 256, 64
P = 128
HALF = C // 2
GROUPS = C // 2
YW = 4


class Stage:

    def __init__(self, nc, stage):
        self.nc, self.stage, self.stack = nc, stage, ExitStack()

    def __enter__(self):
        return self

    def __exit__(self, *error):
        return self.stack.__exit__(*error)

    def sbuf(self, name, shape, dt=F32):
        return self.stack.enter_context(self.nc.sbuf_tensor(f"{self.stage}_{name}", shape, dt))

    def psum(self, name, shape, dt=F32):
        return self.stack.enter_context(self.nc.psum_tensor(f"{self.stage}_{name}", shape, dt))

    def sem(self, name):
        return self.stack.enter_context(self.nc.semaphore(f"{self.stage}_{name}"))


SEED = 8


class Event:

    def __init__(self, sem, step=1, seed=SEED):
        self.sem, self.step, self.seed = sem, step, seed

    def done(self, t):
        return (t + (1 + self.seed)) * self.step


def seed(nc, events):
    with nc.Block() as block:
        @block.sync
        def _(sp):
            for e in events:
                sp.sem_inc(e.sem, e.seed * e.step)


def combine_statistics(nc, stage, stats, n, chunks, chunk_count, averaging, mean, rstd, eps):
    with Stage(nc, stage) as p:
        avg = p.sbuf("averaging", [P, P])
        part = p.sbuf("partial", [P, n])
        dev = p.sbuf("deviation", [P, n, chunks])
        var = p.sbuf("variance", [P, n])
        eps_t = p.sbuf("eps", [P, 1])
        ps = p.psum("averages", [P, 2, n])
        loaded, step, averaged, rooted = (p.sem(s) for s in ("loaded", "step", "averaged", "rooted"))
        with nc.Block() as block:
            @block.sync
            def _(sp):
                sp.dma_start(avg[:], averaging).then_inc(loaded, 16)

            @block.tensor
            def _(pe):
                pe.wait_ge(loaded, 16)
                pe.wait_ge(step, 2)
                nc.tensor.matmul(ps[:, 0, :], avg[:], part[:], start=True, stop=True).then_inc(averaged, 1)
                pe.wait_ge(step, 7)
                nc.tensor.matmul(ps[:, 1, :], avg[:], part[:], start=True, stop=True).then_inc(averaged, 1)

            @block.vector
            def _(v):
                nc.vector.memset(eps_t[:], eps).then_inc(step, 1)
                nc.vector.tensor_reduce(part[:], stats[:, :, :, 1], AX.X, ALU.add).then_inc(step, 1)
                v.wait_ge(averaged, 1)
                nc.vector.tensor_copy(mean, ps[:, 0, :]).then_inc(step, 1)
                v.wait_ge(step, 3)
                nc.vector.tensor_tensor(dev[:], stats[:, :, :, 1], mean.unsqueeze(2).to_broadcast([P, n, chunks]),
                                        ALU.subtract).then_inc(step, 1)
                v.wait_ge(step, 4)
                nc.vector.tensor_tensor(dev[:], dev[:], dev[:], ALU.mult).then_inc(step, 1)
                v.wait_ge(step, 5)
                nc.vector.scalar_tensor_tensor(out=dev[:], in0=stats[:, :, :, 2], scalar=1.0 / chunk_count,
                                               in1=dev[:], op0=ALU.mult, op1=ALU.add).then_inc(step, 1)
                v.wait_ge(step, 6)
                nc.vector.tensor_reduce(part[:], dev[:], AX.X, ALU.add).then_inc(step, 1)
                v.wait_ge(rooted, 1)
                nc.vector.reciprocal(rstd, var[:])

            @block.scalar
            def _(a):
                a.wait_ge(averaged, 2)
                nc.scalar.activation(var[:], ps[:, 1, :], ACT.Sqrt, bias=eps_t[:, 0:1]).then_inc(rooted, 1)


def input_statistics(nc, x, averaging, mean, rstd):
    B = x.shape[0]
    n = 2 * B
    with Stage(nc, "stats") as p:
        stats = p.sbuf("bn", [P, B, GROUPS, 2, 6])
        with Stage(nc, "statsrows") as q:
            rows = q.sbuf("rows", [P, 2, W, C])
            loaded = [q.sem(f"loaded{i}") for i in range(2)]
            used = q.sem("used")
            with nc.Block() as block:
                @block.sync
                def _(sp):
                    for k in range(n):
                        if k >= 2:
                            sp.wait_ge(used, k - 1)
                        sp.dma_start(rows[:, k % 2], x[k // 2, (k % 2) * P:(k % 2 + 1) * P]).then_inc(loaded[k % 2], 16)

                @block.vector
                def _(v):
                    for k in range(n):
                        v.wait_ge(loaded[k % 2], 16 * (k // 2 + 1))
                        for g in range(GROUPS):
                            last = nc.vector.bn_stats(stats[:, k // 2, g, k % 2, :], rows[:, k % 2, :, 2 * g:2 * g + 2])
                        last.then_inc(used, 1)
        combine_statistics(nc, "statsx", stats[:].rearrange("p b g k (e s) -> p (b g) (k e) s", s=3), B * GROUPS, 4, W,
                           averaging, mean, rstd, 1e-5)


def project(nc, x, cat, y, ident_d, proj_wT, proj_b2, averaging1, mean1, rstd1):
    B = x.shape[0]
    WQ = 32
    TILES = 2 * WQ // 8
    ROUNDS = B * W // WQ
    STRIPS = W // WQ
    with Stage(nc, "projstats") as s:
        stats = s.sbuf("bn", [P, B * 2 * W // 8, 6])
        with Stage(nc, "proj") as p:
            raw = [[p.sbuf(f"raw{k}{i}", [P, WQ, C]) for k in range(2)] for i in range(2)]
            src = [p.sbuf(f"src{i}", [P, WQ, 2, C]) for i in range(2)]
            ident = p.sbuf("ident", [P, P])
            weights = p.sbuf("weights", [P, C])
            bias = p.sbuf("bias", [P, 1])
            chans = [p.sbuf(f"chans{i}", [P, 8, P]) for i in range(2)]
            ys = [p.sbuf(f"ys{i}", [P, WQ, 64]) for i in range(2)]
            pt = [p.psum(f"pt{i}", [P, 8, P]) for i in range(2)]
            py = [p.psum(f"py{i}", [P, 8, 64]) for i in range(2)]
            const, passed_sp, passed_q = (p.sem(k) for k in ("const", "passed_sp", "passed_q"))
            loaded = [Event(p.sem(f"loaded{i}"), 32) for i in range(2)]
            stored = [Event(p.sem(f"stored{i}"), 16) for i in range(2)]
            beside = [Event(p.sem(f"beside{i}")) for i in range(2)]
            turned, copied_a, copied_v, mixed, y_ready, counted = (
                Event(p.sem(k)) for k in ("turned", "copied_a", "copied_v", "mixed", "y_ready", "counted"))
            seed(nc, loaded + stored + beside + [turned, copied_a, copied_v, mixed, y_ready, counted])

            def rounds(engine, body, skewed=False):
                with engine.Fori(0, ROUNDS - 1) as i:
                    body(i, False)
                body(ROUNDS - 1, True)

            def place(half, k, i, engine, copy):
                engine.wait_ge(loaded[half].sem, loaded[half].done(i))
                engine.wait_ge(turned.sem, turned.done((i - 1) * TILES + (half + 1) * (TILES // 2) - 1))
                if k == 0:
                    engine.sem_inc(passed_q, 1)
                copy(src[half][:, :, k, :], raw[half][k][:]).then_inc(beside[k].sem, 1)

            with nc.Block() as block:
                @block.sync
                def _(sp):
                    sp.dma_start(ident[:], ident_d).then_inc(const, 16)
                    sp.dma_start(weights[:], proj_wT).then_inc(const, 16)
                    sp.dma_start(bias[:], proj_b2).then_inc(const, 16)
                    with sp.Fori(0, ROUNDS) as i:
                        for half in range(2):
                            sp.wait_ge(beside[0].sem, beside[0].done(i * 2 + half - 2))
                            sp.wait_ge(beside[1].sem, beside[1].done(i * 2 + half - 2))
                            sp.sem_inc(passed_sp, 1)
                            for k, t in enumerate((cat, x)):
                                sp.dma_start(raw[half][k][:],
                                             t[bass.ds(i // STRIPS, 1), half * P:(half + 1) * P, bass.ds((i % STRIPS) * WQ, WQ)]
                                             .rearrange("a p w c -> (a p) w c")).then_inc(loaded[half].sem, 16)

                @block.tensor
                def _(pe):
                    def turn(i, k):
                        t = i * TILES + k
                        half, w0 = k // (TILES // 2), (k % (TILES // 2)) * 8
                        if k % (TILES // 2) == 0:
                            for e in beside:
                                pe.wait_ge(e.sem, e.done(i * 2 + half))
                        pe.wait_ge(copied_a.sem, copied_a.done(t - 2))
                        pe.wait_ge(copied_v.sem, copied_v.done(t - 2))
                        for w in range(8):
                            last = nc.tensor.transpose(pt[k % 2][:, w, :], src[half][:, w0 + w].rearrange("p s c -> p (s c)"), ident[:])
                        last.then_inc(turned.sem, 1)

                    def mix(i, k):
                        t = i * TILES + k
                        pe.wait_ge(copied_a.sem, copied_a.done(t))
                        pe.wait_ge(copied_v.sem, copied_v.done(t))
                        pe.wait_ge(y_ready.sem, y_ready.done(t - 2))
                        for parity in range(2):
                            last = nc.tensor.matmul(
                                py[k % 2][64 * parity:64 * parity + 64, :, :], weights[:],
                                chans[k % 2][:].rearrange("p w (h two) -> p w h two", two=2)[:, :, :, parity],
                                start=True, stop=True)
                        last.then_inc(mixed.sem, 1)

                    def body(i, last):
                        for k in range(TILES):
                            if k + 1 < TILES:
                                turn(i, k + 1)
                            elif not last:
                                turn(i + 1, 0)
                            mix(i, k)
                    pe.wait_ge(const, 48)
                    turn(0, 0)
                    rounds(pe, body)

                @block.gpsimd
                def _(q):
                    with q.Fori(0, ROUNDS) as i:
                        for half in range(2):
                            place(half, 0, i, q, nc.gpsimd.tensor_copy)

                @block.scalar
                def _(a):
                    def copy(i, k):
                        t = i * TILES + k
                        a.wait_ge(turned.sem, turned.done(t))
                        a.wait_ge(mixed.sem, mixed.done(t - 2))
                        nc.scalar.copy(chans[k % 2][:, 0:4, :], pt[k % 2][:, 0:4, :]).then_inc(copied_a.sem, 1)

                    def body(i, last):
                        for k in range(TILES):
                            if k + 1 < TILES:
                                copy(i, k + 1)
                            elif not last:
                                copy(i + 1, 0)
                            half, w0 = k // (TILES // 2), (k % (TILES // 2)) * 8
                            t = i * TILES + k
                            a.wait_ge(mixed.sem, mixed.done(t))
                            if w0 == 0:
                                a.wait_ge(stored[half].sem, stored[half].done(i - 1))
                                a.wait_ge(counted.sem, counted.done((i - 1) * TILES + k + TILES // 2 - 1))
                            nc.scalar.activation(ys[half][:, w0:w0 + 8, :], py[k % 2][:],
                                                 ACT.Identity, bias=bias[:, 0:1]).then_inc(y_ready.sem, 1)
                            if w0 + 8 == WQ:
                                a.wait_ge(y_ready.sem, y_ready.done(t))
                                a.dma_start(y[bass.ds((i % STRIPS) * (WQ // YW), WQ // YW), :, bass.ds(i // STRIPS, 1), half]
                                            .rearrange("w p a v h -> p (w a) (v h)"),
                                            ys[half][:].rearrange("p (w v) h -> p w (v h)", v=YW)).then_inc(stored[half].sem, 16)
                    a.wait_ge(const, 48)
                    copy(0, 0)
                    rounds(a, body)
                    for half in range(2):
                        a.wait_ge(stored[half].sem, stored[half].done(ROUNDS - 1))

                @block.vector
                def _(v):
                    def copy(i, k):
                        t = i * TILES + k
                        v.wait_ge(turned.sem, turned.done(t))
                        v.wait_ge(mixed.sem, mixed.done(t - 2))
                        nc.vector.tensor_copy(chans[k % 2][:, 4:8, :], pt[k % 2][:, 4:8, :]).then_inc(copied_v.sem, 1)

                    def body(i, last):
                        for k in range(TILES):
                            if k + 1 < TILES:
                                copy(i, k + 1)
                            elif not last:
                                copy(i + 1, 0)
                            half, w0 = k // (TILES // 2), (k % (TILES // 2)) * 8
                            t = i * TILES + k
                            if k % (TILES // 2) == 0:
                                if half == 0:
                                    place(1, 1, i, v, nc.vector.tensor_copy)
                                elif not last:
                                    place(0, 1, i + 1, v, nc.vector.tensor_copy)
                            v.wait_ge(y_ready.sem, y_ready.done(t))
                            nc.vector.bn_stats(
                                stats[:, bass.ds(t, 1), :].rearrange("p a s -> p (a s)"),
                                ys[half][:, w0:w0 + 8, :].rearrange("p w h -> p (w h)")).then_inc(counted.sem, 1)
                    place(0, 1, 0, v, nc.vector.tensor_copy)
                    copy(0, 0)
                    rounds(v, body)
        combine_statistics(nc, "projx", stats[:].rearrange("p (b t) (e s) -> p b (t e) s", s=3, b=B), B, 2 * 2 * W // 8,
                           W, averaging1, mean1, rstd1, 1e-5)


def scan(nc, y, out, ident_d, conv_w, conv_b, mean1, rstd1):
    B = y.shape[2]
    BH = B // 2
    H2 = H // 2
    UN = 16
    ROUNDS = W // UN
    with Stage(nc, "scan") as p:
        yb = [p.sbuf(f"y{i}", [P, B, 2, YW, H2 // 2]) for i in range(2)]
        z = [p.sbuf(f"z{i}", [P, B, H2]) for i in range(2)]
        u = [p.sbuf(f"u{i}", [P, BH, H2 + 2]) for i in range(2)]
        g = [p.sbuf(f"g{i}", [P, B, H2]) for i in range(2)]
        o = [p.sbuf(f"o{i}", [P, B, H2]) for i in range(2)]
        outb = [p.sbuf(f"out{i}", [P, 2 * B, 8, C]) for i in range(2)]
        ident = p.sbuf("ident", [P, P])
        cw = p.sbuf("cw", [P, 3, P])
        cb = p.sbuf("cb", [P, 1])
        shift = p.sbuf("shift", [P, B])
        pc = [p.psum(f"conv{i}", [P, BH, H2]) for i in range(2)]
        po = [[p.psum(f"turned{i}{c}", [P, BH, P]) for c in range(2)] for i in range(2)]
        const, cleared, shifted, passed_sp = (p.sem(k) for k in ("const", "cleared", "shifted", "passed_sp"))
        conv, relu, u_ready, z_ready, o_ready, turned, fetched = (
            [Event(p.sem(f"{k}{c}")) for c in range(2)]
            for k in ("conv", "relu", "u_ready", "z_ready", "o_ready", "turned", "fetched"))
        loaded = [Event(p.sem(f"loaded{i}"), 16) for i in range(2)]
        stored = [Event(p.sem(f"stored{i}"), 16 * B) for i in range(2)]
        seed(nc, conv + relu + u_ready + z_ready + o_ready + turned + fetched + loaded + stored)
        with nc.Block() as block:
            @block.sync
            def _(sp):
                sp.dma_start(ident[:], ident_d).then_inc(const, 16)
                sp.dma_start(cw[:], conv_w).then_inc(const, 16)
                sp.dma_start(cb[:], conv_b).then_inc(const, 16)
                with sp.Fori(0, ROUNDS) as i:
                    for k in range(0, UN, YW):
                        for c in range(2):
                            sp.wait_ge(o_ready[c].sem, o_ready[c].done(i * UN + k - YW - 1))
                        sp.sem_inc(passed_sp, 1)
                        sp.dma_start(yb[k // YW % 2][:].rearrange("p b r v h -> p (b r v h)"),
                                     y[bass.ds((W - 1 - k) // YW - i * (UN // YW), 1)]
                                     .rearrange("a p b r v h -> (a p) (b r v h)")).then_inc(loaded[k // YW % 2].sem, 16)

            @block.vector
            def _(v):
                def column(k, b0, b1):
                    return yb[k // YW % 2][:, b0:b1, :, YW - 1 - k % YW, :].rearrange("p b r h -> p (b r) h")

                def normalise(t, k, c, first):
                    if c == 0 and k % YW == 0:
                        v.wait_ge(loaded[k // YW % 2].sem, first)
                    for b in range(c * BH, (c + 1) * BH):
                        last = nc.vector.tensor_scalar(z[k % 2][:, b].rearrange("p (r h) -> p r h", r=2), column(k, b, b + 1), rstd1[:, b:b + 1],
                                                       shift[:, b:b + 1], ALU.mult, ALU.add)
                    last.then_inc(z_ready[c].sem, 1)

                def add(t, k, c):
                    half = slice(c * BH, (c + 1) * BH)
                    v.wait_ge(z_ready[c].sem, z_ready[c].done(t))
                    v.wait_ge(relu[c].sem, relu[c].done(t - 1))
                    nc.vector.tensor_tensor(u[c][:, :, 1:H2 + 1], z[k % 2][:, half], g[(k + 1) % 2][:, half],
                                            ALU.add).then_inc(u_ready[c].sem, 1)

                def result(t, k, c):
                    half = slice(c * BH, (c + 1) * BH)
                    v.wait_ge(relu[c].sem, relu[c].done(t))
                    v.wait_ge(turned[c].sem, turned[c].done(t - 2))
                    wide = lambda t: t.rearrange("p b (r h) -> p (b r) h", r=2)
                    nc.vector.tensor_tensor(wide(o[k % 2][:, half]), column(k % UN, c * BH, (c + 1) * BH), wide(g[k % 2][:, half]),
                                            ALU.add).then_inc(o_ready[c].sem, 1)

                for t in (g[1], u[0], u[1]):
                    nc.vector.memset(t[:], 0.0).then_inc(cleared, 1)
                v.wait_ge(cleared, 3)
                nc.vector.scalar_tensor_tensor(out=shift[:], in0=mean1, scalar=-1.0, in1=rstd1,
                                               op0=ALU.mult, op1=ALU.mult).then_inc(shifted, 1)
                v.wait_ge(shifted, 1)

                def body(i, k, before, after):
                    t = i * UN + k
                    for c in range(2):
                        add(t, k, c)
                        if before:
                            result(t - 1, (k - 1) % UN, c)
                        if after:
                            n = (k + 1) % UN
                            at = i * (UN // YW // 2) + (k + 1) // YW // 2
                            normalise(t + 1, n, c, loaded[n // YW % 2].done(at))
                for c in range(2):
                    normalise(0, 0, c, loaded[0].done(0))
                for k in range(UN):
                    body(0, k, k > 0, True)
                with v.Fori(1, ROUNDS - 1) as i:
                    for k in range(UN):
                        body(i, k, True, True)
                for k in range(UN):
                    body(ROUNDS - 1, k, True, k + 1 < UN)
                for c in range(2):
                    result(W - 1, UN - 1, c)

            @block.tensor
            def _(pe):
                def convolve(t, c):
                    pe.wait_ge(u_ready[c].sem, u_ready[c].done(t))
                    for d in range(3):
                        last = nc.tensor.matmul(pc[c][:], cw[:, d, :], u[c][:, :, d:d + H2], start=(d == 0), stop=(d == 2))
                    last.then_inc(conv[c].sem, 1)

                def turn(t, k, c):
                    pe.wait_ge(o_ready[c].sem, o_ready[c].done(t))
                    pe.wait_ge(fetched[c].sem, fetched[c].done(t - 2))
                    for b in range(BH):
                        last = nc.tensor.transpose(po[k % 2][c][:, b, :], o[k % 2][:, c * BH + b, :], ident[:])
                    last.then_inc(turned[c].sem, 1)

                def body(t, k, before):
                    for c in range(2):
                        convolve(t, c)
                        if before:
                            turn(t - 2, k, c)
                pe.wait_ge(const, 48)
                for k in range(UN):
                    body(k, k, k > 1)
                with pe.Fori(1, ROUNDS) as i:
                    for k in range(UN):
                        body(i * UN + k, k, True)
                for t in (W, W + 1):
                    for c in range(2):
                        turn(t - 2, t, c)

            @block.scalar
            def _(a):
                def rectify(t, k, c):
                    half = slice(c * BH, (c + 1) * BH)
                    a.wait_ge(conv[c].sem, conv[c].done(t))
                    a.wait_ge(o_ready[c].sem, o_ready[c].done(t - 2))
                    nc.scalar.activation(g[k % 2][:, half], pc[c][:], ACT.Relu, bias=cb[:, 0:1]).then_inc(relu[c].sem, 1)

                def fetch(i, k, c):
                    t = i * UN + k
                    a.wait_ge(turned[c].sem, turned[c].done(t))
                    block_, w = k // 8, 7 - k % 8
                    if k % 8 == 0 and c == 0:
                        a.wait_ge(stored[block_].sem, stored[block_].done(i - 1))
                    nc.scalar.copy(outb[block_][:, 2 * c * BH:2 * (c + 1) * BH, w, :],
                                   po[k % 2][c][:].rearrange("p b (r c) -> p (b r) c", r=2)).then_inc(
                        fetched[c].sem, 1)
                    if k % 8 == 7 and c == 1:
                        a.wait_ge(fetched[0].sem, fetched[0].done(t))
                        a.wait_ge(fetched[1].sem, fetched[1].done(t))
                        w0 = W - 8 - 8 * block_ - i * UN
                        for b in range(B):
                            a.dma_start(out[b].rearrange("(h r) w c -> h r w c", r=2)[:, :, bass.ds(w0, 8), :],
                                        outb[block_][:, 2 * b:2 * b + 2]).then_inc(stored[block_].sem, 16)

                def body(i, k, before):
                    for c in range(2):
                        rectify(i * UN + k, k, c)
                        if before:
                            fetch(*((i, k - 2) if k >= 2 else (i - 1, k + UN - 2)), c)

                a.wait_ge(const, 48)
                for k in range(UN):
                    body(0, k, k > 1)
                with a.Fori(1, ROUNDS) as i:
                    for k in range(UN):
                        body(i, k, True)
                for k in (UN - 2, UN - 1):
                    for c in range(2):
                        fetch(ROUNDS - 1, k, c)
                for s in stored:
                    a.wait_ge(s.sem, s.done(ROUNDS - 1))


WIN, HEADS, HC = 8, 4, 8


def local_mixer(nc, x, cat, ident_d, wq_d, wk_d, wv_d, bq_d, bk_d, bv_d, pos_d, mask_d, onehot_d, mean0, rstd0):
    B = x.shape[0]
    NT = B * H // (2 * WIN)
    SLABS = H // (2 * WIN)
    with Stage(nc, "attn") as p:
        xt = [p.sbuf(f"xt{i}", [P, 2, 2, WIN, C]) for i in range(2)]
        xr = p.sbuf("xr", [P, WIN, P])
        xn = p.sbuf("xn", [P, 16, 64])
        kst = [p.sbuf(f"kst{i}", [P, 8, 64]) for i in range(2)]
        qb = [[p.sbuf(f"qb{t}{s}", [P, 16, P]) for s in range(2)] for t in range(2)]
        kb = [[p.sbuf(f"kb{t}{s}", [P, 16, HEADS, 64]) for s in range(2)] for t in range(2)]
        vb = [p.sbuf(f"vb{t}", [P, 16, 2, 8, HC + 1]) for t in range(2)]
        ident, wq, wk, wv = (p.sbuf(k, [P, P]) for k in ("ident", "wq", "wk", "wv"))
        bq, bk = (p.sbuf(k, [P, 1]) for k in ("bq", "bk"))
        bqs = p.sbuf("bqs", [P, 1])
        bv = p.sbuf("bv", [P, 2, 8, HC])
        mask = p.sbuf("mask", [P, HEADS])
        row = p.sbuf("row", [1, 2, B, P])
        one = p.sbuf("one", [1, 1])
        affine = p.sbuf("affine", [P, 2, B])
        mx = [p.sbuf(f"mx{i}", [P, 16]) for i in range(2)]
        ss = [p.sbuf(f"ss{i}", [P, 16, 64]) for i in range(4)]
        pts = [p.sbuf(f"pts{i}", [P, 8, P]) for i in range(2)]
        rz = p.sbuf("rz", [P, 16])
        lo = [p.sbuf(f"lo{i}", [P, 32, 32]) for i in range(2)]
        ps = [p.psum(f"scores{i}", [P, 4, 256]) for i in range(2)]
        pt = p.psum("turned", [P, 8, P])
        po = p.psum("outputs", [P, 16, 2, HC + 1])
        pb = p.psum("prepare", [P, 512])
        const, init, passed_sp, row_ready, spread, passed_q, passed_a = (
            p.sem(k) for k in ("const", "init", "passed_sp", "row_ready", "spread", "passed_q", "passed_a"))
        x_loaded = [Event(p.sem(f"x_loaded{i}"), 16 * 2) for i in range(2)]
        stored = [[Event(p.sem(f"stored{i}{s}"), 16 * 2 * WIN) for s in range(2)] for i in range(2)]
        xr_ready, turned, xn_ready, k_made, k_staged, k_ready, q_made, q_ready, v_made, v_ready = (
            Event(p.sem(k)) for k in ("xr_ready", "x_turned", "xn_ready", "k_made", "k_staged", "k_ready", "q_made",
                                      "q_ready", "v_made", "v_ready"))
        scored, max_ready, less_ready, exp_ready, p_turned, p_a, p_v, o_made, sum_ready, o_ready = (
            Event(p.sem(k)) for k in ("scored", "max_ready", "less_ready", "exp_ready", "p_turned", "p_a", "p_v", "o_made",
                                      "sum_ready", "o_ready"))
        seed(nc, x_loaded + stored[0] + stored[1] + [xr_ready, turned, xn_ready, k_made, k_staged, k_ready, q_made, q_ready, v_made,
                                      v_ready, scored, max_ready, less_ready, exp_ready, p_turned, p_a, p_v, o_made,
                                      sum_ready, o_ready])

        def nxt(m, k):
            return (m, 1) if k == 0 else (m + 1, 0)

        def ahead(m, k, c, by):
            if c + by < 0:
                m, k = (m, 0) if k == 1 else (m - 1, 1)
            elif c + by >= 8:
                m, k = nxt(m, k)
            return m, k, (c + by) % 8

        def tiles(engine, body):
            for k in range(2):
                body(0, k, True, True)
            with engine.Fori(1, NT // 2 - 1) as m:
                for k in range(2):
                    body(m, k, True, True)
            body(NT // 2 - 1, 0, True, False)
            body(NT // 2 - 1, 1, False, False)

        def first_later(m, k):
            return not (isinstance(m, int) and m == 0 and k == 0)

        CONSTS = 9 + 2 * 2 * (16 + 16)
        with nc.Block() as block:
            @block.sync
            def _(sp):
                for t, d in ((ident, ident_d), (wq, wq_d), (wk, wk_d), (wv, wv_d), (bq, bq_d), (bk, bk_d), (bv, bv_d),
                             (mask, mask_d), (one, ident_d[0:1, 0:1])):
                    sp.dma_start(t[:], d).then_inc(const, 16)
                for t in range(2):
                    for s in range(2):
                        fixed = slice(64, 128) if s == 0 else slice(0, 64)
                        for w in range(16):
                            sp.dma_start(qb[t][s][fixed, w], onehot_d).then_inc(const, 16)
                            sp.dma_start(kb[t][s][fixed, w], pos_d).then_inc(const, 16)

                def load(m, k):
                    T = m * 2 + k
                    sp.wait_ge(xr_ready.sem, xr_ready.done(T - 2))
                    sp.sem_inc(passed_sp, 1)
                    for s in range(2):
                        rows = x[bass.ds(T // SLABS, 1), bass.ds((T % SLABS) * 16 + s * 8, 8)] if not isinstance(T, int) else \
                            x[T // SLABS:T // SLABS + 1, (T % SLABS) * 16 + s * 8:(T % SLABS) * 16 + s * 8 + 8]
                        sp.dma_start(xt[k][:, s].rearrange("p a v c -> p (a v c)"),
                                     rows.rearrange("a h (q v) c -> (a h) q (v c)", q=16)).then_inc(x_loaded[k].sem, 16)

                def store(m, k):
                    T = m * 2 + k
                    sp.wait_ge(o_ready.sem, o_ready.done(T * 8 + 7))
                    sp.sem_inc(passed_sp, 1)
                    for s in range(2):
                        rows = cat[bass.ds(T // SLABS, 1), bass.ds((T % SLABS) * 16 + s * 8, 8), :, 0:HALF] if not isinstance(T, int) \
                            else cat[T // SLABS:T // SLABS + 1, (T % SLABS) * 16 + s * 8:(T % SLABS) * 16 + s * 8 + 8, :, 0:HALF]
                        for a_ in range(2):
                            dst = rows.rearrange("a h (q w v) c -> w (a h) v q c", q=16, w=2)[a_]
                            for h in range(WIN):
                                r = 64 * a_ + WIN * h
                                sp.dma_start(dst[h], lo[k][r:r + WIN, 16 * s:16 * s + 16]).then_inc(stored[k][s].sem, 16)

                def body(m, k, n1, n2):
                    if n2:
                        load(m + 1, k)
                    store(m, k)
                load(0, 0)
                load(0, 1)
                tiles(sp, body)
                for k in range(2):
                    for s in range(2):
                        sp.wait_ge(stored[k][s].sem, stored[k][s].done(NT // 2 - 1))

            @block.gpsimd
            def _(q):
                def copy(m, k):
                    T = m * 2 + k
                    q.wait_ge(x_loaded[k].sem, x_loaded[k].done(m))
                    q.wait_ge(turned.sem, turned.done(T * 2 - 1))
                    q.wait_ge(k_ready.sem, k_ready.done((T - 1) * 2 + 1))
                    q.sem_inc(passed_q, 1)
                    for s in range(2):
                        last = nc.gpsimd.tensor_copy(
                            xr[:, :, 64 * s:64 * s + 64].rearrange("p v (a c) -> p v a c", a=2),
                            xt[k][:, s, :, :, 0:HALF].rearrange("p a v c -> p v a c"))
                    last.then_inc(xr_ready.sem, 1)

                def keys(m, k):
                    T = m * 2 + k
                    for half in range(2):
                        q.wait_ge(k_staged.sem, k_staged.done(T * 2 + half))
                        for s in range(2):
                            r = slice(64 * s, 64 * s + 64)
                            last = nc.gpsimd.tensor_tensor(
                                kb[k][s][r, 8 * half:8 * half + 8],
                                kst[half][r].unsqueeze(2).to_broadcast([64, 8, HEADS, 64]),
                                mask[r].unsqueeze(1).unsqueeze(3).to_broadcast([64, 8, HEADS, 64]), ALU.mult)
                        last.then_inc(k_ready.sem, 1)
                q.wait_ge(const, 16 * CONSTS)
                copy(0, 0)
                keys(0, 0)
                copy(0, 1)

                def body(m, k, n1, n2):
                    if n1:
                        keys(*nxt(m, k))
                    if n2:
                        copy(m + 1, k)
                tiles(q, body)

            @block.tensor
            def _(pe):
                def prepare(m, k, piece):
                    T = m * 2 + k
                    half = piece % 2
                    before = (v_ready.done(T * 2 - 1), xn_ready.done(T * 2), xn_ready.done(T * 2 + 1), k_staged.done(T * 2),
                              k_staged.done(T * 2 + 1), q_ready.done(T * 2), q_ready.done(T * 2 + 1), v_ready.done(T * 2))[piece]
                    pe.wait_ge((v_ready, xn_ready, xn_ready, k_staged, k_staged, q_ready, q_ready, v_ready)[piece].sem, before)
                    if piece < 2:
                        pe.wait_ge(xr_ready.sem, xr_ready.done(T))
                        for v_ in range(4):
                            last = nc.tensor.transpose(pb[:, 128 * v_:128 * v_ + 128], xr[:, 4 * half + v_, :], ident[:])
                        last.then_inc(turned.sem, 1)
                    elif piece < 6:
                        last = nc.tensor.matmul(pb[:], (wk if piece < 4 else wq)[:],
                                                xn[:, 8 * half:8 * half + 8].rearrange("p q t -> p (q t)"), start=True, stop=True)
                        last.then_inc((k_made if piece < 4 else q_made).sem, 1)
                    else:
                        for j in range(4):
                            w = 8 * half + 2 * j
                            last = nc.tensor.matmul(pb[:, 128 * j:128 * j + 128], xn[:, w:w + 2].rearrange("p q t -> p (q t)"),
                                                    wv[:], start=True, stop=True)
                        last.then_inc(v_made.sem, 1)

                def scores(m, k, c):
                    g, T = (m * 2 + k) * 8 + c, m * 2 + k
                    s, w0 = c // 4, 4 * (c % 4)
                    if c == 0:
                        pe.wait_ge(k_ready.sem, k_ready.done(T * 2 + 1))
                        pe.wait_ge(q_ready.sem, q_ready.done(T * 2 + 1))
                    pe.wait_ge(less_ready.sem, less_ready.done(g - 2))
                    for w in range(4):
                        last = nc.tensor.matmul(ps[c % 2][:, w], qb[k][s][:, w0 + w],
                                                kb[k][s][:, w0 + w].rearrange("p h t -> p (h t)"), start=True, stop=True)
                    last.then_inc(scored.sem, 1)

                def turn(m, k, c):
                    g = (m * 2 + k) * 8 + c
                    pe.wait_ge(exp_ready.sem, exp_ready.done(g))
                    pe.wait_ge(p_a.sem, p_a.done(g - 1))
                    pe.wait_ge(p_v.sem, p_v.done(g - 1))
                    e = ss[c % 4][:].rearrange("p (w h) t -> p w (h t)", w=8)
                    for w in range(8):
                        last = nc.tensor.transpose(pt[:, w, :], e[:, w, :], ident[:])
                    last.then_inc(p_turned.sem, 1)

                def outputs(m, k, c):
                    g, T = (m * 2 + k) * 8 + c, m * 2 + k
                    s, w0 = c // 4, 4 * (c % 4)
                    pe.wait_ge(p_a.sem, p_a.done(g))
                    pe.wait_ge(p_v.sem, p_v.done(g))
                    pe.wait_ge(v_ready.sem, v_ready.done(T * 2 + 1))
                    pe.wait_ge(o_ready.sem, o_ready.done(g - 1))
                    for w in range(4):
                        for hp in range(2):
                            v_ = vb[k][:, w0 + w].rearrange("p e (s a h) c -> p e s a h c", s=2, a=2)[:, :, s, :, hp]
                            e0 = 4 * w + 2 * hp
                            last = nc.tensor.matmul(po[:, e0:e0 + 2], pts[c % 2][:, 2 * w + hp], v_, start=True, stop=True)
                    last.then_inc(o_made.sem, 1)

                pe.wait_ge(const, 16 * CONSTS)
                pe.wait_ge(row_ready, 2)
                for a_ in range(2):
                    for b in range(B):
                        last = nc.tensor.matmul(po[:].rearrange("p e a c -> p (e a c)")[:, a_ * B + b:a_ * B + b + 1],
                                                row[0:1, a_, b, :], one[:], start=True, stop=True)
                last.then_inc(spread, 1)
                pe.wait_ge(init, 1)
                for piece in range(8):
                    prepare(0, 0, piece)
                scores(0, 0, 0)
                scores(0, 0, 1)

                def body(m, k, n1, n2):
                    for c in range(8):
                        if c < 6 or n1:
                            scores(*ahead(m, k, c, 2))
                        turn(m, k, c)
                        if n1:
                            prepare(*nxt(m, k), c)
                        if c > 0 or first_later(m, k):
                            outputs(*ahead(m, k, c, -1))
                tiles(pe, body)
                outputs(NT // 2 - 1, 1, 7)

            @block.scalar
            def _(a):
                def prepare(m, k, piece):
                    T = m * 2 + k
                    half = piece % 2
                    b = T // SLABS
                    if piece < 2:
                        a.wait_ge(turned.sem, turned.done(T * 2 + half))
                        if half == 0:
                            a.wait_ge(v_made.sem, v_made.done(T * 2 - 1))
                        a.sem_inc(passed_a, 1)
                        sc, bi = (affine[:, j, b:b + 1] if isinstance(b, int) else affine[:, j, bass.ds(b, 1)] for j in range(2))
                        for v_ in range(4):
                            last = nc.scalar.activation(
                                xn[:].rearrange("p q (h v) -> p h q v", v=WIN)[:, :, :, 4 * half + v_],
                                pb[:, 128 * v_:128 * v_ + 128].rearrange("p (h q) -> p h q", h=WIN), ACT.Identity, bias=bi, scale=sc)
                        last.then_inc(xn_ready.sem, 1)
                    elif piece < 4:
                        a.wait_ge(k_made.sem, k_made.done(T * 2 + half))
                        a.wait_ge(k_ready.sem, k_ready.done(T * 2 - 2 + half))
                        nc.scalar.activation(kst[half][:].rearrange("p q t -> p (q t)"), pb[:], ACT.Identity,
                                             bias=bk[:, 0:1]).then_inc(k_staged.sem, 1)
                    elif piece < 6:
                        a.wait_ge(q_made.sem, q_made.done(T * 2 + half))
                        for s in range(2):
                            for w in range(2):
                                r = slice(64 * s + 32 * w, 64 * s + 32 * w + 32)
                                last = nc.scalar.activation(qb[k][s][r, 8 * half:8 * half + 8, 64 * w:64 * w + 64],
                                                            pb[r].rearrange("p (q t) -> p q t", q=8), ACT.Identity,
                                                            bias=bqs[r, 0:1], scale=HC ** -0.5)
                        last.then_inc(q_ready.sem, 1)

                def exponentials(m, k, c):
                    g = (m * 2 + k) * 8 + c
                    a.wait_ge(less_ready.sem, less_ready.done(g))
                    nc.scalar.activation(ss[c % 4][:], ss[c % 4][:], ACT.Exp).then_inc(exp_ready.sem, 1)

                def fetch(m, k, c):
                    g = (m * 2 + k) * 8 + c
                    a.wait_ge(p_turned.sem, p_turned.done(g))
                    a.wait_ge(o_made.sem, o_made.done(g - 2))
                    nc.scalar.copy(pts[c % 2][:, 0:4], pt[:, 0:4]).then_inc(p_a.sem, 1)

                a.wait_ge(const, 16 * CONSTS)
                a.wait_ge(init, 1)
                for piece in range(8):
                    prepare(0, 0, piece)
                exponentials(0, 0, 0)

                def body(m, k, n1, n2):
                    for c in range(8):
                        if c < 7 or n1:
                            exponentials(*ahead(m, k, c, 1))
                        fetch(m, k, c)
                        if n1:
                            prepare(*nxt(m, k), c)
                tiles(a, body)

            @block.vector
            def _(v):
                def values(m, k, half):
                    T = m * 2 + k
                    v.wait_ge(v_made.sem, v_made.done(T * 2 + half))
                    for odd in range(2):
                        src = slice(64 * odd, 64 * odd + 64)
                        for hh in range(2):
                            dst = slice(64 * hh, 64 * hh + 64)
                            last = nc.vector.tensor_tensor(
                                vb[k][dst, 8 * half + odd:8 * half + 8:2, hh, :, 0:HC],
                                pb[src].rearrange("p (j e s c) -> p j e s c", j=4, e=2, c=HC)[:, :, hh],
                                bv[src, hh].unsqueeze(1).to_broadcast([64, 4, 8, HC]), ALU.add)
                    last.then_inc(v_ready.sem, 1)

                def maxima(m, k, c):
                    g = (m * 2 + k) * 8 + c
                    s_ = ps[c % 2][:].rearrange("p w (h t) -> p (w h) t", t=64)
                    v.wait_ge(scored.sem, scored.done(g))
                    nc.vector.tensor_reduce(mx[c % 2][:], s_, AX.X, ALU.max).then_inc(max_ready.sem, 1)
                    v.wait_ge(max_ready.sem, max_ready.done(g))
                    v.wait_ge(p_turned.sem, p_turned.done(g - 2))
                    nc.vector.tensor_tensor(ss[c % 4][:], s_, mx[c % 2][:].unsqueeze(2).to_broadcast([P, 16, 64]),
                                            ALU.subtract).then_inc(less_ready.sem, 1)

                def fetch(m, k, c):
                    g = (m * 2 + k) * 8 + c
                    v.wait_ge(p_turned.sem, p_turned.done(g))
                    v.wait_ge(o_made.sem, o_made.done(g - 2))
                    nc.vector.tensor_copy(pts[c % 2][:, 4:8], pt[:, 4:8]).then_inc(p_v.sem, 1)

                def normalise(m, k, c):
                    g = (m * 2 + k) * 8 + c
                    v.wait_ge(o_made.sem, o_made.done(g))
                    if c % 4 == 0:
                        v.wait_ge(stored[k][c // 4].sem, stored[k][c // 4].done(m - 1))
                    v.wait_ge(o_ready.sem, o_ready.done(g - 1))
                    for w in range(2):
                        r = slice(64 * w, 64 * w + 64)
                        last = nc.vector.reciprocal(rz[r], po[r, :, w, HC])
                    last.then_inc(sum_ready.sem, 1)
                    v.wait_ge(sum_ready.sem, sum_ready.done(g))
                    for w in range(2):
                        r = slice(64 * w, 64 * w + 64)
                        last = nc.vector.tensor_tensor(
                            lo[k][r, 4 * c:4 * c + 4].rearrange("p q (h c) -> p (q h) c", c=HC), po[r, :, w, 0:HC],
                            rz[r].unsqueeze(2).to_broadcast([64, 16, HC]), ALU.mult)
                    last.then_inc(o_ready.sem, 1)

                v.wait_ge(const, 16 * CONSTS)
                ng = HALF // 2
                mr = mean0.rearrange("p (b g) -> p b g", b=B)[0:1, :, 0:ng]
                rr = rstd0.rearrange("p (b g) -> p b g", b=B)[0:1, :, 0:ng]
                out_ = lambda a_, b: row[0:1, a_, b].rearrange("p (s g e) -> p s g e", s=4, e=2)
                wide = lambda t, b: t[:, b:b + 1].unsqueeze(3).to_broadcast([1, 4, ng, 2])
                for b in range(B):
                    last = nc.vector.tensor_copy(out_(0, b), wide(rr, b))
                    last = nc.vector.tensor_copy(out_(1, b), wide(mr, b))
                last.then_inc(row_ready, 1)
                v.wait_ge(row_ready, 1)
                nc.vector.scalar_tensor_tensor(out=row[0:1, 1].rearrange("p b c -> p (b c)"), in0=row[0:1, 1].rearrange("p b c -> p (b c)"),
                                               scalar=-1.0, in1=row[0:1, 0].rearrange("p b c -> p (b c)"),
                                               op0=ALU.mult, op1=ALU.mult).then_inc(row_ready, 1)
                for t in range(2):
                    for s in range(2):
                        for w in range(2):
                            r = slice(64 * s + 32 * w, 64 * s + 32 * w + 32)
                            nc.vector.memset(qb[t][s][r, :, 64 * (1 - w):64 * (1 - w) + 64], 0.0)
                    for hh in range(2):
                        r = slice(64 * hh, 64 * hh + 64)
                        nc.vector.memset(vb[t][r, :, 1 - hh], 0.0)
                        nc.vector.memset(vb[t][r, :, hh, :, HC:HC + 1], 1.0)
                nc.vector.tensor_scalar(bqs[:], bq[:], HC ** -0.5, None, ALU.mult)
                v.wait_ge(spread, 1)
                nc.vector.tensor_copy(affine[:].rearrange("p a b -> p (a b)"),
                                      po[:].rearrange("p e a c -> p (e a c)")[:, 0:2 * B]).then_inc(init, 1)
                for half in range(2):
                    values(0, 0, half)
                maxima(0, 0, 0)
                maxima(0, 0, 1)

                def body(m, k, n1, n2):
                    for c in range(8):
                        if c > 1 or first_later(m, k):
                            normalise(*ahead(m, k, c, -2))
                        if c < 6 or n1:
                            maxima(*ahead(m, k, c, 2))
                        fetch(m, k, c)
                        if n1 and c >= 6:
                            values(*nxt(m, k), c - 6)
                tiles(v, body)
                for c in (6, 7):
                    normalise(NT // 2 - 1, 1, c)


KH = H // 2 + 1
NI = 4
MAGIC = 1.5 * 2 ** 23
TWO_PI = 6.2831850


def global_mixer(nc, x, cat, dft, params, mean0, rstd0):
    B = x.shape[0]
    NG = B * HALF // NI
    GB = HALF // NI
    with Stage(nc, "mix") as p:
        xs = p.sbuf("images", [P, 2, 2, W, HALF])
        consts = {k: p.sbuf(k, list(v.shape)) for k, v in dft.items()}
        par = {k: p.sbuf(k, list(v.shape)) for k, v in params.items()}
        cospb = p.sbuf("cospb", [P, HALF])
        folded = [p.sbuf(f"folded{i}", [P, 2, W]) for i in range(2)]
        half1 = p.sbuf("half1", [P, 257])
        rows = [p.sbuf(f"rows{i}", [P, 2, 2 * KH]) for i in range(2)]
        re = [p.sbuf(f"re{i}", [P, NI, 2, KH]) for i in range(2)]
        im = [p.sbuf(f"im{i}", [P, NI, 2, KH]) for i in range(2)]
        b0, b1, b2, b3, b4, b5, ga, gb = (p.sbuf(k, [P, NI, 2, KH]) for k in
                                          ("sum", "tangent", "amp", "angle", "sine", "cosine", "ga", "gb"))
        half3 = p.sbuf("half3", [P, 2, 128])
        cols = [p.sbuf(f"cols{i}", [P, 2, W]) for i in range(2)]
        quarter = p.sbuf("quarter", [P, 2])
        p1 = p.psum("p1", [P, 2, 512])
        p2 = p.psum("p2", [P, 2, 512])
        p3 = [p.psum(f"p3{i}", [P, 2, 256]) for i in range(2)]
        p4 = [p.psum(f"p4{i}", [P, 2, W]) for i in range(2)]
        const, init, passed_sp, passed_q, passed_a = (p.sem(k) for k in ("const", "init", "passed_sp", "passed_q", "passed_a"))
        x_loaded, x_stored = (Event(p.sem(k), 32) for k in ("x_loaded", "x_stored"))
        fold_ready, rows_made, half1_ready, rows_ready, spec_made, spec_ready = (
            Event(p.sem(k)) for k in ("fold_ready", "rows_made", "half1_ready", "rows_ready", "spec_made", "spec_ready"))
        cols_made, half3_ready, cols_ready, image_made, image_ready = (
            Event(p.sem(k)) for k in ("cols_made", "half3_ready", "cols_ready", "image_made", "image_ready"))
        ACT_STEPS, DVE_STEPS, POOL_STEPS = 6, 19, 11
        act_step, dve_step, pool_step = (Event(p.sem(k), seed=60) for k in ("act_step", "dve_step", "pool_step"))
        seed(nc, [x_loaded, x_stored, fold_ready, rows_made, half1_ready, rows_ready, spec_made, spec_ready, cols_made,
                  half3_ready, cols_ready, image_made, image_ready, act_step, dve_step, pool_step])
        flat = lambda t: t[:].rearrange("p a b c -> p (a b c)")

        def columns(t, at, size=1):
            return t[:, at:at + size] if isinstance(at, int) else t[:, bass.ds(at, size)]

        def pipeline(engine, body):
            body(-1, True, False, False, 1)
            body(0, True, True, False, 0)
            with engine.Fori(0, (NG - 4) // 2) as i:
                for k in range(2):
                    body(i * 2 + (1 + k), True, True, True, (1 + k) % 2)
            for n in (NG - 3, NG - 2):
                body(n, True, True, True, n % 2)
            body(NG - 1, False, True, True, (NG - 1) % 2)
            body(NG, False, False, True, NG % 2)

        with nc.Block() as block:
            @block.sync
            def _(sp):
                for k in consts:
                    sp.dma_start(consts[k][:], dft[k]).then_inc(const, 16)
                for k in par:
                    sp.dma_start(par[k][:], params[k]).then_inc(const, 16)

                def load(b, buf):
                    for hh in range(2):
                        sp.dma_start(xs[:, bass.ds(buf, 1), hh].rearrange("p a w c -> p (a w) c"),
                                     x[bass.ds(b, 1), hh * P:(hh + 1) * P, :, HALF:C].rearrange("a p w c -> (a p) w c")
                                     ).then_inc(x_loaded.sem, 16)

                def store(b, buf):
                    sp.wait_ge(image_ready.sem, image_ready.done(b * HALF + HALF - 1))
                    sp.sem_inc(passed_sp, 1)
                    for hh in range(2):
                        sp.dma_start(cat[bass.ds(b, 1), hh * P:(hh + 1) * P, :, HALF:C].rearrange("a p w c -> (a p) w c"),
                                     xs[:, bass.ds(buf, 1), hh].rearrange("p a w c -> p (a w) c")).then_inc(x_stored.sem, 16)
                load(0, 0)
                with sp.Fori(0, B - 1) as b:
                    sp.wait_ge(x_loaded.sem, x_loaded.done(b))
                    sp.wait_ge(x_stored.sem, x_stored.done(b - 1))
                    sp.sem_inc(passed_sp, 1)
                    load(b + 1, (b + 1) % 2)
                    store(b, b % 2)
                store(B - 1, (B - 1) % 2)
                sp.wait_ge(x_stored.sem, x_stored.done(B - 1))

            @block.tensor
            def _(pe):
                pe.wait_ge(const, 16 * (len(consts) + len(par)))

                def row_product(t, j):
                    f = folded[j % 2]
                    pe.wait_ge(fold_ready.sem, fold_ready.done(t))
                    pe.wait_ge(rows_ready.sem, rows_ready.done(t - 1))
                    for wh in range(2):
                        e, o = f[:, 0, wh * P:(wh + 1) * P], f[:, 1, wh * P:(wh + 1) * P]
                        nc.tensor.matmul(p1[:, wh, 0:64], e, consts["rows_even"][:, 0:64], start=True, stop=True)
                        nc.tensor.matmul(p1[:, wh, 128:193], e, consts["rows_even"][:, 64:129], start=True, stop=True)
                        last = nc.tensor.matmul(p1[:, wh, 64:322].rearrange("p (s k) -> p s k", s=2)[:, :, 0:64], o,
                                                consts["rows_odd"][:].rearrange("p (s k) -> p s k", s=2), start=True, stop=True)
                    last.then_inc(rows_made.sem, 1)

                def column_product(t, j):
                    r = rows[j % 2]
                    pe.wait_ge(rows_ready.sem, rows_ready.done(t))
                    pe.wait_ge(spec_ready.sem, spec_ready.done(t - 1))
                    for q in range(2):
                        c, s, ms = (consts["columns"][:, 3 * q + k, :] for k in range(3))
                        nc.tensor.matmul(p2[:, q, 0:2 * KH], c, r[:, q, :], start=True, stop=False)
                        nc.tensor.matmul(p2[:, q, 0:KH], s, r[:, q, KH:2 * KH], start=False, stop=False)
                        last = nc.tensor.matmul(p2[:, q, KH:2 * KH], ms, r[:, q, 0:KH], start=False, stop=True)
                    last.then_inc(spec_made.sem, 1)

                def column_product_back(u, j):
                    pe.wait_ge(cols_ready.sem, cols_ready.done(u - 2))
                    for q in range(2):
                        c, s, ms = ((consts["columns"] if q == 0 else consts["columns_back"])[:, k, :] for k in range(3))
                        a_, b_ = ga[:, j, q, :], gb[:, j, q, :]
                        nc.tensor.matmul(p3[j % 2][:, q, 0:128], a_[:, 1:KH], c, start=True, stop=False)
                        nc.tensor.matmul(p3[j % 2][:, q, 0:128], b_[:, 1:KH], ms, start=False, stop=True)
                        nc.tensor.matmul(p3[j % 2][:, q, 128:256], a_[:, 0:128], s, start=True, stop=False)
                        last = nc.tensor.matmul(p3[j % 2][:, q, 128:256], b_[:, 0:128], c, start=False, stop=True)
                    last.then_inc(cols_made.sem, 1)

                def row_product_back(u, j):
                    pe.wait_ge(cols_ready.sem, cols_ready.done(u))
                    pe.wait_ge(image_ready.sem, image_ready.done(u - 2))
                    for hh in range(2):
                        nc.tensor.matmul(p4[j % 2][:, hh, :], consts["rows_back"][:, 0, hh * P:(hh + 1) * P], cols[j % 2][:, 0, :],
                                         start=True, stop=False)
                        last = nc.tensor.matmul(p4[j % 2][:, hh, :], consts["rows_back"][:, 1, hh * P:(hh + 1) * P],
                                                cols[j % 2][:, 1, :], start=False, stop=True)
                    last.then_inc(image_made.sem, 1)

                def body(n, fwd, point, inv, parity):
                    for j in range(NI):
                        t, u = (n + 1) * NI + j, (n - 1) * NI + j
                        if fwd:
                            row_product(t, j)
                        if inv:
                            if j == 0:
                                pe.wait_ge(pool_step.sem, pool_step.done(n * POOL_STEPS - 1))
                            column_product_back(u, j)
                        if fwd:
                            column_product(t, j)
                        if inv:
                            row_product_back(u, j)
                pipeline(pe, body)

            @block.scalar
            def _(a):
                a.wait_ge(const, 16 * (len(consts) + len(par)))
                a.wait_ge(init, 4)
                nc.scalar.activation(cospb[:], cospb[:], ACT.Sin, scale=-TWO_PI, bias=quarter[:, 0:1]).then_inc(init, 1)

                def step(n, k, ins):
                    ins.then_inc(act_step.sem, 1)

                def body(n, fwd, point, inv, parity):
                    RE, IM = flat(re[parity]), flat(im[parity])
                    for j in range(NI):
                        t, u = (n + 1) * NI + j, (n - 1) * NI + j
                        if fwd:
                            a.wait_ge(rows_made.sem, rows_made.done(t))
                            a.wait_ge(rows_ready.sem, rows_ready.done(t - 1))
                            nc.scalar.copy(half1[:], p1[:, 1, 0:257]).then_inc(half1_ready.sem, 1)
                        if inv:
                            a.wait_ge(cols_made.sem, cols_made.done(u))
                            a.wait_ge(cols_ready.sem, cols_ready.done(u - 1))
                            nc.scalar.copy(half3[:].rearrange("p a b -> p (a b)"), p3[j % 2][:, 1, :]).then_inc(half3_ready.sem, 1)
                        if point:
                            if j == 0:
                                a.wait_ge(pool_step.sem, pool_step.done((n - 1) * POOL_STEPS + POOL_STEPS - 1))
                                a.wait_ge(spec_ready.sem, spec_ready.done(n * NI + NI - 1))
                                step(n, 0, nc.scalar.activation(flat(b0), RE, ACT.Square))
                                step(n, 1, nc.scalar.activation(flat(b1), IM, ACT.Square))
                            elif j == 1:
                                a.wait_ge(pool_step.sem, pool_step.done(n * POOL_STEPS + 0))
                                step(n, 2, nc.scalar.activation(flat(b2), flat(b0), ACT.Sqrt, bias=quarter[:, 1:2]))
                            elif j == 2:
                                a.wait_ge(dve_step.sem, dve_step.done(n * DVE_STEPS + 3))
                                step(n, 3, nc.scalar.activation(flat(b3), flat(b1), ACT.Arctan))
                            else:
                                a.wait_ge(dve_step.sem, dve_step.done(n * DVE_STEPS + 15))
                                step(n, 4, nc.scalar.activation(flat(b4), flat(b1), ACT.Sin, scale=TWO_PI))
                                a.wait_ge(dve_step.sem, dve_step.done(n * DVE_STEPS + 16))
                                step(n, 5, nc.scalar.activation(flat(b5), flat(b0), ACT.Sin, scale=-TWO_PI, bias=quarter[:, 0:1]))
                        if fwd:
                            a.wait_ge(spec_made.sem, spec_made.done(t))
                            if j == 0:
                                a.wait_ge(pool_step.sem, pool_step.done((n - 1) * POOL_STEPS + 4))
                                a.wait_ge(dve_step.sem, dve_step.done((n - 1) * DVE_STEPS + 3))
                            nc.scalar.copy(re[1 - parity][:, j], p2[:, :, 0:KH])
                            nc.scalar.copy(im[1 - parity][:, j], p2[:, :, KH:2 * KH]).then_inc(spec_ready.sem, 1)
                        if inv:
                            a.wait_ge(image_made.sem, image_made.done(u))
                            a.sem_inc(passed_a, 1)
                            nc.scalar.activation(image_out(n, j), p4[j % 2][:], ACT.Abs).then_inc(image_ready.sem, 1)

                def image_out(n, j):
                    if isinstance(n, int):
                        return xs[:, ((n - 1) // GB) % 2, :, :, ((n - 1) % GB) * NI + j]
                    m = n - 1
                    return xs[:, bass.ds((m // GB) % 2, 1), :, :, bass.ds((m % GB) * NI + j, 1)].rearrange(
                        "p a h w c -> p (a h) (w c)")
                pipeline(a, body)

            @block.gpsimd
            def _(q):
                def step(n, k, ins):
                    ins.then_inc(pool_step.sem, 1)

                def own(n, k):
                    q.wait_ge(pool_step.sem, pool_step.done(n * POOL_STEPS + k))

                def body(n, fwd, point, inv, parity):
                    if not point:
                        return
                    RE, IM = flat(re[parity]), flat(im[parity])
                    tt, ts = nc.gpsimd.tensor_tensor, nc.gpsimd.tensor_scalar
                    q.wait_ge(act_step.sem, act_step.done(n * ACT_STEPS + 1))
                    step(n, 0, tt(flat(b0), flat(b0), flat(b1), ALU.add))
                    q.wait_ge(dve_step.sem, dve_step.done((n - 1) * DVE_STEPS + DVE_STEPS - 1))
                    own(n, 0)
                    q.sem_inc(passed_q, 1)
                    step(n, 1, ts(flat(b4), RE, 0.0, None, ALU.is_lt))
                    step(n, 2, ts(flat(b5), IM, 0.0, -0.5, ALU.is_ge, ALU.add))
                    own(n, 2)
                    step(n, 3, tt(flat(b5), flat(b5), flat(b4), ALU.mult))
                    own(n, 3)
                    q.sem_inc(passed_q, 1)
                    step(n, 4, ts(flat(b4), flat(b4), -2.0 / np.pi, 1.0 / np.pi, ALU.mult, ALU.add))
                    q.wait_ge(dve_step.sem, dve_step.done(n * DVE_STEPS + 1))
                    q.sem_inc(passed_q, 1)
                    amp = b2[:].rearrange("p n a b -> p n (a b)")
                    for k, (name, op) in enumerate((("amp_w", ALU.mult), ("amp_b", ALU.add))):
                        by = columns(par[name], (n if name == "amp_w" else n % GB) * NI, NI)
                        step(n, 5 + k, tt(amp, amp, by.unsqueeze(2).to_broadcast([P, NI, 2 * KH]), op))
                        own(n, 5 + k)
                    chs = columns(cospb, (n % GB) * NI, NI)
                    for k, at in enumerate((0, 64)):
                        step(n, 7 + k, tt(b2[at:at + 1, :, 0, 1:128], b2[at:at + 1, :, 0, 1:128],
                                          chs[at:at + 1].unsqueeze(2).to_broadcast([1, NI, 127]), ALU.mult))
                    for k, g_ in enumerate((ga, gb)):
                        q.wait_ge(dve_step.sem, dve_step.done(n * DVE_STEPS + 17 + k))
                        step(n, 9 + k, tt(g_[:].rearrange("p n a b -> p n (a b)"), g_[:].rearrange("p n a b -> p n (a b)"),
                                           consts["offset"][:, k:k + 1, :].to_broadcast([P, NI, 2 * KH]), ALU.add))
                q.wait_ge(init, 5)
                pipeline(q, body)

            @block.vector
            def _(v):
                v.wait_ge(const, 16 * (len(consts) + len(par)))
                tt, ts, stt = nc.vector.tensor_tensor, nc.vector.tensor_scalar, nc.vector.scalar_tensor_tensor
                nc.vector.memset(quarter[:, 0:1], float(np.pi / 2)).then_inc(init, 1)
                nc.vector.memset(quarter[:, 1:2], 1e-30)
                nc.vector.memset(rows[0][:], 0.0)
                nc.vector.memset(rows[1][:], 0.0)
                pbt = par["pha_b"]
                ts(pbt[:], pbt[:], float(1 / (2 * np.pi)), None, ALU.mult).then_inc(init, 1)
                v.wait_ge(init, 2)
                ts(cospb[:], pbt[:], MAGIC, MAGIC, ALU.add, ALU.subtract).then_inc(init, 1)
                v.wait_ge(init, 3)
                tt(cospb[:], pbt[:], cospb[:], ALU.subtract).then_inc(fold_init := p.sem("fold_init"), 1)
                v.wait_ge(fold_init, 1)
                g0 = HALF // 2
                up = lambda t: t.rearrange("p (b g) -> p b g", b=B)[:, :, g0:].unsqueeze(3).to_broadcast([P, B, g0, 2])
                aw = par["amp_w"][:].rearrange("p (b g two) -> p b g two", b=B, two=2)
                m2 = p.sbuf("mean2", [P, B * HALF])
                for b in range(B):
                    tt(aw[:, b], aw[:, b], up(rstd0)[:, b], ALU.mult)
                    ts(m2[:].rearrange("p (b g two) -> p b g two", b=B, two=2)[:, b], up(mean0)[:, b], -2.0, None, ALU.mult)
                stt(out=cospb[:], in0=cospb[:], scalar=-1.0, in1=cospb[:], op0=ALU.mult, op1=ALU.max).then_inc(init, 1)
                v.wait_ge(init, 4)
                v.drain()

                def fold_rows(n, j):
                    t = n * NI + j
                    if isinstance(n, int):
                        src = xs[:, (n // GB) % 2, :, :, (n % GB) * NI + j]
                    else:
                        src = xs[:, bass.ds((n // GB) % 2, 1), :, :, bass.ds((n % GB) * NI + j, 1)].rearrange(
                            "p a h w c -> p (a h) (w c)")
                    m = columns(m2, t)
                    v.wait_ge(x_loaded.sem, x_loaded.done(n // GB))
                    v.wait_ge(rows_made.sem, rows_made.done(t - 2))
                    stt(out=folded[j % 2][:, 0], in0=src[:, 0], scalar=m, in1=src[:, 1], op0=ALU.add, op1=ALU.add)
                    tt(folded[j % 2][:, 1], src[:, 0], src[:, 1], ALU.subtract).then_inc(fold_ready.sem, 1)

                def step(n, k, ins):
                    ins.then_inc(dve_step.sem, 1)

                def own(n, k):
                    v.wait_ge(dve_step.sem, dve_step.done(n * DVE_STEPS + k))

                def body(n, fwd, point, inv, parity):
                    RE, IM = flat(re[parity]), flat(im[parity])
                    for j in range(NI):
                        t, u = (n + 1) * NI + j, (n - 1) * NI + j
                        if fwd:
                            if n == -1 and j == 0 if isinstance(n, int) else False:
                                fold_rows(0, 0)
                            v.wait_ge(half1_ready.sem, half1_ready.done(t))
                            v.wait_ge(spec_made.sem, spec_made.done(t - 2))
                            tt(rows[j % 2][:, 0, 0:257], p1[:, 0, 0:257], half1[:], ALU.add)
                            tt(rows[j % 2][:, 1, 0:257], p1[:, 0, 0:257], half1[:], ALU.subtract).then_inc(rows_ready.sem, 1)
                        if inv:
                            v.wait_ge(half3_ready.sem, half3_ready.done(u))
                            v.wait_ge(image_made.sem, image_made.done(u - 2))
                            e = p3[j % 2][:, 0, :].rearrange("p (s w) -> p s w", s=2)
                            tt(cols[j % 2][:, :, 0:128], e, half3[:], ALU.add)
                            tt(cols[j % 2][:, :, 128:256], e, half3[:], ALU.subtract).then_inc(cols_ready.sem, 1)
                        if fwd:
                            if j + 1 < NI:
                                fold_rows(n + 1, j + 1)
                            elif not (isinstance(n, int) and n + 2 >= NG):
                                fold_rows(n + 2, 0)
                        if point:
                            if j == 1:
                                v.wait_ge(act_step.sem, act_step.done(n * ACT_STEPS + 2))
                                step(n, 0, stt(out=flat(b0), in0=RE, scalar=-1.0, in1=RE, op0=ALU.mult, op1=ALU.max))
                                own(n, 0)
                                step(n, 1, tt(flat(b0), flat(b0), flat(b2), ALU.add))
                                own(n, 1)
                                step(n, 2, nc.vector.reciprocal(flat(b0), flat(b0)))
                                own(n, 2)
                                step(n, 3, tt(flat(b1), IM, flat(b0), ALU.mult))
                            elif j == 2:
                                v.wait_ge(act_step.sem, act_step.done(n * ACT_STEPS + 3))
                                v.wait_ge(pool_step.sem, pool_step.done(n * POOL_STEPS + 4))
                                step(n, 4, tt(flat(b3), flat(b3), flat(b4), ALU.mult))
                                own(n, 4)
                                step(n, 5, tt(flat(b3), flat(b3), flat(b5), ALU.add))
                                own(n, 5)
                                for i_ in range(NI):
                                    col = lambda t_: columns(t_, (n % GB) * NI + i_)
                                    w_ = lambda t_: t_[:, i_].rearrange("p a b -> p (a b)")
                                    step(n, 6 + i_, stt(out=w_(b1), in0=w_(b3), scalar=col(par["pha_w"]),
                                                        in1=consts["turn"][:, 1, :], op0=ALU.mult, op1=ALU.add))
                                own(n, 9)
                                for i_ in range(NI):
                                    col = lambda t_: columns(t_, (n % GB) * NI + i_)
                                    w_ = lambda t_: t_[:, i_].rearrange("p a b -> p (a b)")
                                    step(n, 10 + i_, stt(out=w_(b1), in0=consts["turn"][:, 0, :], scalar=col(pbt),
                                                        in1=w_(b1), op0=ALU.mult, op1=ALU.add))
                                own(n, 13)
                                step(n, 14, ts(flat(b0), flat(b1), MAGIC, MAGIC, ALU.add, ALU.subtract))
                                own(n, 14)
                                step(n, 15, tt(flat(b1), flat(b1), flat(b0), ALU.subtract))
                                own(n, 15)
                                step(n, 16, stt(out=flat(b0), in0=flat(b1), scalar=-1.0, in1=flat(b1), op0=ALU.mult, op1=ALU.max))
                            elif j == 3:
                                v.wait_ge(pool_step.sem, pool_step.done(n * POOL_STEPS + 8))
                                v.wait_ge(cols_made.sem, cols_made.done((n - 1) * NI + NI - 1))
                                v.wait_ge(act_step.sem, act_step.done(n * ACT_STEPS + 5))
                                step(n, 17, tt(flat(ga), flat(b2), flat(b5), ALU.mult))
                                step(n, 18, tt(flat(gb), flat(b2), flat(b4), ALU.mult))
                pipeline(v, body)


def constants():
    ch = np.arange(P)
    group1 = (ch[:, None] % C // 2 == ch[None, :] % C // 2).astype(np.float32)
    i = np.arange(P)
    rest = np.concatenate([np.arange(2, 128, 2), np.arange(1, 128, 2)])
    cos = lambda a, b: np.cos(2 * np.pi * ((a[:, None] * b[None, :]) % W) / W)
    sin = lambda a, b: np.where((a[:, None] * b[None, :]) % 128 == 0, 0.0, np.sin(2 * np.pi * ((a[:, None] * b[None, :]) % W) / W))
    even, odd = rest[:63], rest[63:]
    z = np.zeros((P, 1))
    col = lambda k: np.array([k])
    kw = [2 * i, 2 * i + 1]
    h = np.arange(H)
    side = [np.where((k == 0) | (k == 128), 0.0, np.where(k < 128, 1.0, -1.0)) for k in kw]
    turn = np.zeros((P, 2, 2, KH))
    offset = np.zeros((P, 2, 2, KH))
    for q in range(2):
        turn[:, 0, q, :] = side[q][:, None]
        turn[:, 1, q, 0] = 0.25
        offset[:, 0, q, :] = 2e-8
        offset[:, 0, q, 0] = -1e-8 * side[q]
        offset[:, 1, q, :] = 1e-8 * side[q][:, None]
        offset[:, 1, q, 0] = 2e-8
    turn[[0, 64], 0, 0, 0] = turn[[0, 64], 0, 0, KH - 1] = 1.0
    dft = {
        "rows_even": np.concatenate([cos(i, col(128)), cos(i, even), cos(i, col(0)), z, -sin(i, even)], 1),
        "rows_odd": np.concatenate([cos(i, odd), -sin(i, odd)], 1),
        "columns": np.stack([m for k in kw for m in (cos(i, k), sin(i, k), -sin(i, k))], 1),
        "columns_back": np.stack([cos(kw[1], i), sin(kw[1], i), -sin(kw[1], i)], 1),
        "rows_back": np.stack([np.concatenate([2 * cos(rest, h), cos(col(0), h)]),
                               np.concatenate([cos(col(128), h), -2 * sin(rest, h)])], 1) / (H * W),
        "turn": turn.reshape(P, 2, 2 * KH),
        "offset": offset.reshape(P, 2, 2 * KH),
    }
    head = (np.arange(P)[:, None] % HALF) // HC == np.arange(HEADS)[None, :]
    return {
        "mask": head.astype(np.float32),
        "onehot": np.concatenate([np.eye(64), np.eye(64)], 1).astype(np.float32),
        "dft": {k: np.ascontiguousarray(m, np.float32) for k, m in dft.items()},
        "ident": np.eye(P, dtype=np.float32),
        "avg0": np.full((P, P), 1.0 / (P * 4), np.float32),
        "avg1": group1 * np.float32(1.0 / (4 * 2 * 2 * W // 8)),
    }


def attention_layout(w_qkv, b_qkv):
    q, k, v = (w_qkv[HALF * i:HALF * i + HALF] for i in range(3))

    def diagonal(m):
        out = np.zeros((4, HALF, 4, HALF), m.dtype)
        for i in range(4):
            out[i, :, i, :] = m.T
        return out
    wv = diagonal(v).reshape(4, HALF, 4, 2, 2, HC).transpose(0, 1, 4, 2, 3, 5)
    bq, bk, bv = (b_qkv[HALF * i:HALF * i + HALF] for i in range(3))
    return (np.ascontiguousarray(diagonal(q).reshape(P, P)), np.ascontiguousarray(diagonal(k).reshape(P, P)),
            np.ascontiguousarray(wv.reshape(P, P)), np.tile(bq, 4)[:, None].copy(), np.tile(bk, 4)[:, None].copy(),
            np.ascontiguousarray(np.broadcast_to(bv.reshape(2, 2, HC).transpose(1, 0, 2)[None, :, None], (P, 2, 4, 2, HC))).reshape(P, 2, 8, HC))


def conv_layout(w):
    m = np.zeros((2, C, 3, 2, C), w.dtype)
    for d in range(3):
        for pi in range(2):
            for po in range(2):
                tap = 2 * (d - 1) + pi - po + 2
                if 0 <= tap < 5:
                    m[pi, :, d, po, :] = w[:, tap, 0, :]
    return np.ascontiguousarray(m.reshape(P, 3, P))


def build(nc, out, x, params, dft, **a):
    B = x.shape[0]
    cat = nc.dram_tensor("cat", [B, H, W, C], F32).ap()
    y = nc.dram_tensor("y", [W // YW, P, B, 2, YW, H // 4], F32).ap()
    with Stage(nc, "norm") as p:
        mean0, rstd0 = (p.sbuf(k, [P, B * GROUPS])[:] for k in ("mean0", "rstd0"))
        mean1, rstd1 = (p.sbuf(k, [P, B])[:] for k in ("mean1", "rstd1"))
        input_statistics(nc, x, a["avg0"], mean0, rstd0)
        local_mixer(nc, x, cat, a["ident"], a["wq"], a["wk"], a["wv"], a["bq"], a["bk"], a["bv"], a["pos"], a["mask"],
                    a["onehot"], mean0, rstd0)
        global_mixer(nc, x, cat, dft, params, mean0, rstd0)
        project(nc, x, cat, y, a["ident"], a["proj_w"], a["proj_b"], a["avg1"], mean1, rstd1)
        scan(nc, y, out, a["ident"], a["conv_w"], a["conv_b"], mean1, rstd1)


def kernel(x, L0_conv_w_qkv, L0_conv_b_qkv, L0_conv_pos_emb, L0_conv_amp_w, L0_conv_amp_b, L0_conv_pha_w, L0_conv_pha_b,
           L0_conv_proj_w, L0_conv_proj_b, L1_conv_w, L1_conv_b):
    import concourse.bacc as bacc
    from concourse.bass_utils import run_bass_kernel_spmd

    asarray = lambda t: np.ascontiguousarray(np.asarray(t))
    x = asarray(x)
    B = x.shape[0]
    fixed = constants()
    wq, wk, wv, bq, bk, bv = attention_layout(asarray(L0_conv_w_qkv), asarray(L0_conv_b_qkv))
    per_image = lambda t, n: np.ascontiguousarray(np.broadcast_to(np.tile(asarray(t), n), (P, n * HALF)))
    arrays = {
        "x": x, "wq": wq, "wk": wk, "wv": wv, "bq": bq, "bk": bk, "bv": bv,
        "pos": np.ascontiguousarray(asarray(L0_conv_pos_emb)[0].transpose(1, 0, 2)),
        "proj_w": np.concatenate([asarray(L0_conv_proj_w).T, np.eye(C, dtype=np.float32)]),
        "proj_b": np.ascontiguousarray(np.tile(asarray(L0_conv_proj_b), 2)[:, None]),
        "conv_w": conv_layout(asarray(L1_conv_w)),
        "conv_b": np.ascontiguousarray(np.tile(asarray(L1_conv_b), 2)[:, None]),
    }
    arrays |= {k: fixed[k] for k in ("ident", "avg0", "avg1", "mask", "onehot")}
    params = {"amp_w": per_image(L0_conv_amp_w, B), "amp_b": per_image(L0_conv_amp_b, 1),
              "pha_w": per_image(L0_conv_pha_w, 1), "pha_b": per_image(L0_conv_pha_b, 1)}
    nc = bacc.Bacc("TRN2", target_bir_lowering=False, num_devices=1)
    sent = {}

    def declare(prefix, group):
        found = {}
        for k, t in group.items():
            sent[prefix + k] = t
            found[k] = nc.dram_tensor(prefix + k, t.shape, mybir.dt.from_np(t.dtype), kind="ExternalInput").ap()
        return found
    tensors, par, dft = declare("in_", arrays), declare("par_", params), declare("dft_", fixed["dft"])
    out = nc.dram_tensor("out", x.shape, F32, kind="ExternalOutput").ap()
    build(nc, out, params=par, dft=dft, **tensors)
    return run_bass_kernel_spmd(nc, [sent], core_ids=[0]).results[0]["out"]
```

```python
import numpy as np
import concourse.bass as bass
from concourse import mybir
from contextlib import ExitStack

F32 = mybir.dt.float32
ALU = mybir.AluOpType
ACT = mybir.ActivationFunctionType
AX = mybir.AxisListType
H, W, C = 256, 256, 64
P = 128
HALF = C // 2
GROUPS = C // 2
YW = 4


class Stage:

    def __init__(self, nc, stage):
        self.nc, self.stage, self.stack = nc, stage, ExitStack()

    def __enter__(self):
        return self

    def __exit__(self, *error):
        return self.stack.__exit__(*error)

    def sbuf(self, name, shape, dt=F32):
        return self.stack.enter_context(self.nc.sbuf_tensor(f"{self.stage}_{name}", shape, dt))

    def psum(self, name, shape, dt=F32):
        return self.stack.enter_context(self.nc.psum_tensor(f"{self.stage}_{name}", shape, dt))

    def sem(self, name):
        return self.stack.enter_context(self.nc.semaphore(f"{self.stage}_{name}"))


SEED = 8


class Event:

    def __init__(self, sem, step=1, seed=SEED):
        self.sem, self.step, self.seed = sem, step, seed

    def done(self, t):
        return (t + (1 + self.seed)) * self.step


def seed(nc, events):
    with nc.Block() as block:
        @block.sync
        def _(sp):
            for e in events:
                sp.sem_inc(e.sem, e.seed * e.step)


def combine_statistics(nc, stage, stats, n, chunks, chunk_count, averaging, mean, rstd, eps):
    with Stage(nc, stage) as p:
        avg = p.sbuf("averaging", [P, P])
        part = p.sbuf("partial", [P, n])
        dev = p.sbuf("deviation", [P, n, chunks])
        var = p.sbuf("variance", [P, n])
        eps_t = p.sbuf("eps", [P, 1])
        ps = p.psum("averages", [P, 2, n])
        loaded, step, averaged, rooted = (p.sem(s) for s in ("loaded", "step", "averaged", "rooted"))
        with nc.Block() as block:
            @block.sync
            def _(sp):
                sp.dma_start(avg[:], averaging).then_inc(loaded, 16)

            @block.tensor
            def _(pe):
                pe.wait_ge(loaded, 16)
                pe.wait_ge(step, 2)
                nc.tensor.matmul(ps[:, 0, :], avg[:], part[:], start=True, stop=True).then_inc(averaged, 1)
                pe.wait_ge(step, 7)
                nc.tensor.matmul(ps[:, 1, :], avg[:], part[:], start=True, stop=True).then_inc(averaged, 1)

            @block.vector
            def _(v):
                nc.vector.memset(eps_t[:], eps).then_inc(step, 1)
                nc.vector.tensor_reduce(part[:], stats[:, :, :, 1], AX.X, ALU.add).then_inc(step, 1)
                v.wait_ge(averaged, 1)
                nc.vector.tensor_copy(mean, ps[:, 0, :]).then_inc(step, 1)
                v.wait_ge(step, 3)
                nc.vector.tensor_tensor(dev[:], stats[:, :, :, 1], mean.unsqueeze(2).to_broadcast([P, n, chunks]),
                                        ALU.subtract).then_inc(step, 1)
                v.wait_ge(step, 4)
                nc.vector.tensor_tensor(dev[:], dev[:], dev[:], ALU.mult).then_inc(step, 1)
                v.wait_ge(step, 5)
                nc.vector.scalar_tensor_tensor(out=dev[:], in0=stats[:, :, :, 2], scalar=1.0 / chunk_count,
                                               in1=dev[:], op0=ALU.mult, op1=ALU.add).then_inc(step, 1)
                v.wait_ge(step, 6)
                nc.vector.tensor_reduce(part[:], dev[:], AX.X, ALU.add).then_inc(step, 1)
                v.wait_ge(rooted, 1)
                nc.vector.reciprocal(rstd, var[:])

            @block.scalar
            def _(a):
                a.wait_ge(averaged, 2)
                nc.scalar.activation(var[:], ps[:, 1, :], ACT.Sqrt, bias=eps_t[:, 0:1]).then_inc(rooted, 1)


def input_statistics(nc, x, averaging, mean, rstd):
    B = x.shape[0]
    n = 2 * B
    with Stage(nc, "stats") as p:
        stats = p.sbuf("bn", [P, B, GROUPS, 2, 6])
        with Stage(nc, "statsrows") as q:
            rows = q.sbuf("rows", [P, 2, W, C])
            loaded = [q.sem(f"loaded{i}") for i in range(2)]
            used = q.sem("used")
            with nc.Block() as block:
                @block.sync
                def _(sp):
                    for k in range(n):
                        if k >= 2:
                            sp.wait_ge(used, k - 1)
                        sp.dma_start(rows[:, k % 2], x[k // 2, (k % 2) * P:(k % 2 + 1) * P]).then_inc(loaded[k % 2], 16)

                @block.vector
                def _(v):
                    for k in range(n):
                        v.wait_ge(loaded[k % 2], 16 * (k // 2 + 1))
                        for g in range(GROUPS):
                            last = nc.vector.bn_stats(stats[:, k // 2, g, k % 2, :], rows[:, k % 2, :, 2 * g:2 * g + 2])
                        last.then_inc(used, 1)
        combine_statistics(nc, "statsx", stats[:].rearrange("p b g k (e s) -> p (b g) (k e) s", s=3), B * GROUPS, 4, W,
                           averaging, mean, rstd, 1e-5)


def project(nc, x, cat, y, ident_d, proj_wT, proj_b2, averaging1, mean1, rstd1):
    B = x.shape[0]
    WQ = 32
    TILES = 2 * WQ // 8
    ROUNDS = B * W // WQ
    STRIPS = W // WQ
    with Stage(nc, "projstats") as s:
        stats = s.sbuf("bn", [P, B * 2 * W // 8, 6])
        with Stage(nc, "proj") as p:
            raw = [[p.sbuf(f"raw{k}{i}", [P, WQ, C]) for k in range(2)] for i in range(2)]
            src = [p.sbuf(f"src{i}", [P, WQ, 2, C]) for i in range(2)]
            ident = p.sbuf("ident", [P, P])
            weights = p.sbuf("weights", [P, C])
            bias = p.sbuf("bias", [P, 1])
            chans = [p.sbuf(f"chans{i}", [P, 8, P]) for i in range(2)]
            ys = [p.sbuf(f"ys{i}", [P, WQ, 64]) for i in range(2)]
            pt = [p.psum(f"pt{i}", [P, 8, P]) for i in range(2)]
            py = [p.psum(f"py{i}", [P, 8, 64]) for i in range(2)]
            const, passed_sp, passed_q = (p.sem(k) for k in ("const", "passed_sp", "passed_q"))
            loaded = [Event(p.sem(f"loaded{i}"), 32) for i in range(2)]
            stored = [Event(p.sem(f"stored{i}"), 16) for i in range(2)]
            beside = [Event(p.sem(f"beside{i}")) for i in range(2)]
            turned, copied_a, copied_v, mixed, y_ready, counted = (
                Event(p.sem(k)) for k in ("turned", "copied_a", "copied_v", "mixed", "y_ready", "counted"))
            seed(nc, loaded + stored + beside + [turned, copied_a, copied_v, mixed, y_ready, counted])

            def rounds(engine, body, skewed=False):
                with engine.Fori(0, ROUNDS - 1) as i:
                    body(i, False)
                body(ROUNDS - 1, True)

            def place(half, k, i, engine, copy):
                engine.wait_ge(loaded[half].sem, loaded[half].done(i))
                engine.wait_ge(turned.sem, turned.done((i - 1) * TILES + (half + 1) * (TILES // 2) - 1))
                if k == 0:
                    engine.sem_inc(passed_q, 1)
                copy(src[half][:, :, k, :], raw[half][k][:]).then_inc(beside[k].sem, 1)

            with nc.Block() as block:
                @block.sync
                def _(sp):
                    sp.dma_start(ident[:], ident_d).then_inc(const, 16)
                    sp.dma_start(weights[:], proj_wT).then_inc(const, 16)
                    sp.dma_start(bias[:], proj_b2).then_inc(const, 16)
                    with sp.Fori(0, ROUNDS) as i:
                        for half in range(2):
                            sp.wait_ge(beside[0].sem, beside[0].done(i * 2 + half - 2))
                            sp.wait_ge(beside[1].sem, beside[1].done(i * 2 + half - 2))
                            sp.sem_inc(passed_sp, 1)
                            for k, t in enumerate((cat, x)):
                                sp.dma_start(raw[half][k][:],
                                             t[bass.ds(i // STRIPS, 1), half * P:(half + 1) * P, bass.ds((i % STRIPS) * WQ, WQ)]
                                             .rearrange("a p w c -> (a p) w c")).then_inc(loaded[half].sem, 16)

                @block.tensor
                def _(pe):
                    def turn(i, k):
                        t = i * TILES + k
                        half, w0 = k // (TILES // 2), (k % (TILES // 2)) * 8
                        if k % (TILES // 2) == 0:
                            for e in beside:
                                pe.wait_ge(e.sem, e.done(i * 2 + half))
                        pe.wait_ge(copied_a.sem, copied_a.done(t - 2))
                        pe.wait_ge(copied_v.sem, copied_v.done(t - 2))
                        for w in range(8):
                            last = nc.tensor.transpose(pt[k % 2][:, w, :], src[half][:, w0 + w].rearrange("p s c -> p (s c)"), ident[:])
                        last.then_inc(turned.sem, 1)

                    def mix(i, k):
                        t = i * TILES + k
                        pe.wait_ge(copied_a.sem, copied_a.done(t))
                        pe.wait_ge(copied_v.sem, copied_v.done(t))
                        pe.wait_ge(y_ready.sem, y_ready.done(t - 2))
                        for parity in range(2):
                            last = nc.tensor.matmul(
                                py[k % 2][64 * parity:64 * parity + 64, :, :], weights[:],
                                chans[k % 2][:].rearrange("p w (h two) -> p w h two", two=2)[:, :, :, parity],
                                start=True, stop=True)
                        last.then_inc(mixed.sem, 1)

                    def body(i, last):
                        for k in range(TILES):
                            if k + 1 < TILES:
                                turn(i, k + 1)
                            elif not last:
                                turn(i + 1, 0)
                            mix(i, k)
                    pe.wait_ge(const, 48)
                    turn(0, 0)
                    rounds(pe, body)

                @block.gpsimd
                def _(q):
                    with q.Fori(0, ROUNDS) as i:
                        for half in range(2):
                            place(half, 0, i, q, nc.gpsimd.tensor_copy)

                @block.scalar
                def _(a):
                    def copy(i, k):
                        t = i * TILES + k
                        a.wait_ge(turned.sem, turned.done(t))
                        a.wait_ge(mixed.sem, mixed.done(t - 2))
                        nc.scalar.copy(chans[k % 2][:, 0:4, :], pt[k % 2][:, 0:4, :]).then_inc(copied_a.sem, 1)

                    def body(i, last):
                        for k in range(TILES):
                            if k + 1 < TILES:
                                copy(i, k + 1)
                            elif not last:
                                copy(i + 1, 0)
                            half, w0 = k // (TILES // 2), (k % (TILES // 2)) * 8
                            t = i * TILES + k
                            a.wait_ge(mixed.sem, mixed.done(t))
                            if w0 == 0:
                                a.wait_ge(stored[half].sem, stored[half].done(i - 1))
                                a.wait_ge(counted.sem, counted.done((i - 1) * TILES + k + TILES // 2 - 1))
                            nc.scalar.activation(ys[half][:, w0:w0 + 8, :], py[k % 2][:],
                                                 ACT.Identity, bias=bias[:, 0:1]).then_inc(y_ready.sem, 1)
                            if w0 + 8 == WQ:
                                a.wait_ge(y_ready.sem, y_ready.done(t))
                                a.dma_start(y[bass.ds((i % STRIPS) * (WQ // YW), WQ // YW), :, bass.ds(i // STRIPS, 1), half]
                                            .rearrange("w p a v h -> p (w a) (v h)"),
                                            ys[half][:].rearrange("p (w v) h -> p w (v h)", v=YW)).then_inc(stored[half].sem, 16)
                    a.wait_ge(const, 48)
                    copy(0, 0)
                    rounds(a, body)
                    for half in range(2):
                        a.wait_ge(stored[half].sem, stored[half].done(ROUNDS - 1))

                @block.vector
                def _(v):
                    def copy(i, k):
                        t = i * TILES + k
                        v.wait_ge(turned.sem, turned.done(t))
                        v.wait_ge(mixed.sem, mixed.done(t - 2))
                        nc.vector.tensor_copy(chans[k % 2][:, 4:8, :], pt[k % 2][:, 4:8, :]).then_inc(copied_v.sem, 1)

                    def body(i, last):
                        for k in range(TILES):
                            if k + 1 < TILES:
                                copy(i, k + 1)
                            elif not last:
                                copy(i + 1, 0)
                            half, w0 = k // (TILES // 2), (k % (TILES // 2)) * 8
                            t = i * TILES + k
                            if k % (TILES // 2) == 0:
                                if half == 0:
                                    place(1, 1, i, v, nc.vector.tensor_copy)
                                elif not last:
                                    place(0, 1, i + 1, v, nc.vector.tensor_copy)
                            v.wait_ge(y_ready.sem, y_ready.done(t))
                            nc.vector.bn_stats(
                                stats[:, bass.ds(t, 1), :].rearrange("p a s -> p (a s)"),
                                ys[half][:, w0:w0 + 8, :].rearrange("p w h -> p (w h)")).then_inc(counted.sem, 1)
                    place(0, 1, 0, v, nc.vector.tensor_copy)
                    copy(0, 0)
                    rounds(v, body)
        combine_statistics(nc, "projx", stats[:].rearrange("p (b t) (e s) -> p b (t e) s", s=3, b=B), B, 2 * 2 * W // 8,
                           W, averaging1, mean1, rstd1, 1e-5)


def scan(nc, y, out, ident_d, conv_w, conv_b, mean1, rstd1):
    B = y.shape[2]
    BH = B // 2
    H2 = H // 2
    UN = 16
    ROUNDS = W // UN
    with Stage(nc, "scan") as p:
        yb = [p.sbuf(f"y{i}", [P, B, 2, YW, H2 // 2]) for i in range(2)]
        z = [p.sbuf(f"z{i}", [P, B, H2]) for i in range(2)]
        u = [p.sbuf(f"u{i}", [P, BH, H2 + 2]) for i in range(2)]
        g = [p.sbuf(f"g{i}", [P, B, H2]) for i in range(2)]
        o = [p.sbuf(f"o{i}", [P, B, H2]) for i in range(2)]
        outb = [p.sbuf(f"out{i}", [P, 2 * B, 8, C]) for i in range(2)]
        ident = p.sbuf("ident", [P, P])
        cw = p.sbuf("cw", [P, 3, P])
        cb = p.sbuf("cb", [P, 1])
        shift = p.sbuf("shift", [P, B])
        pc = [p.psum(f"conv{i}", [P, BH, H2]) for i in range(2)]
        po = [[p.psum(f"turned{i}{c}", [P, BH, P]) for c in range(2)] for i in range(2)]
        const, cleared, shifted, passed_sp = (p.sem(k) for k in ("const", "cleared", "shifted", "passed_sp"))
        conv, relu, u_ready, z_ready, o_ready, turned, fetched = (
            [Event(p.sem(f"{k}{c}")) for c in range(2)]
            for k in ("conv", "relu", "u_ready", "z_ready", "o_ready", "turned", "fetched"))
        loaded = [Event(p.sem(f"loaded{i}"), 16) for i in range(2)]
        stored = [Event(p.sem(f"stored{i}"), 16 * B) for i in range(2)]
        seed(nc, conv + relu + u_ready + z_ready + o_ready + turned + fetched + loaded + stored)
        with nc.Block() as block:
            @block.sync
            def _(sp):
                sp.dma_start(ident[:], ident_d).then_inc(const, 16)
                sp.dma_start(cw[:], conv_w).then_inc(const, 16)
                sp.dma_start(cb[:], conv_b).then_inc(const, 16)
                with sp.Fori(0, ROUNDS) as i:
                    for k in range(0, UN, YW):
                        for c in range(2):
                            sp.wait_ge(o_ready[c].sem, o_ready[c].done(i * UN + k - YW - 1))
                        sp.sem_inc(passed_sp, 1)
                        sp.dma_start(yb[k // YW % 2][:].rearrange("p b r v h -> p (b r v h)"),
                                     y[bass.ds((W - 1 - k) // YW - i * (UN // YW), 1)]
                                     .rearrange("a p b r v h -> (a p) (b r v h)")).then_inc(loaded[k // YW % 2].sem, 16)

            @block.vector
            def _(v):
                def column(k, b0, b1):
                    return yb[k // YW % 2][:, b0:b1, :, YW - 1 - k % YW, :].rearrange("p b r h -> p (b r) h")

                def normalise(t, k, c, first):
                    if c == 0 and k % YW == 0:
                        v.wait_ge(loaded[k // YW % 2].sem, first)
                    for b in range(c * BH, (c + 1) * BH):
                        last = nc.vector.tensor_scalar(z[k % 2][:, b].rearrange("p (r h) -> p r h", r=2), column(k, b, b + 1), rstd1[:, b:b + 1],
                                                       shift[:, b:b + 1], ALU.mult, ALU.add)
                    last.then_inc(z_ready[c].sem, 1)

                def add(t, k, c):
                    half = slice(c * BH, (c + 1) * BH)
                    v.wait_ge(z_ready[c].sem, z_ready[c].done(t))
                    v.wait_ge(relu[c].sem, relu[c].done(t - 1))
                    nc.vector.tensor_tensor(u[c][:, :, 1:H2 + 1], z[k % 2][:, half], g[(k + 1) % 2][:, half],
                                            ALU.add).then_inc(u_ready[c].sem, 1)

                def result(t, k, c):
                    half = slice(c * BH, (c + 1) * BH)
                    v.wait_ge(relu[c].sem, relu[c].done(t))
                    v.wait_ge(turned[c].sem, turned[c].done(t - 2))
                    wide = lambda t: t.rearrange("p b (r h) -> p (b r) h", r=2)
                    nc.vector.tensor_tensor(wide(o[k % 2][:, half]), column(k % UN, c * BH, (c + 1) * BH), wide(g[k % 2][:, half]),
                                            ALU.add).then_inc(o_ready[c].sem, 1)

                for t in (g[1], u[0], u[1]):
                    nc.vector.memset(t[:], 0.0).then_inc(cleared, 1)
                v.wait_ge(cleared, 3)
                nc.vector.scalar_tensor_tensor(out=shift[:], in0=mean1, scalar=-1.0, in1=rstd1,
                                               op0=ALU.mult, op1=ALU.mult).then_inc(shifted, 1)
                v.wait_ge(shifted, 1)

                def body(i, k, before, after):
                    t = i * UN + k
                    for c in range(2):
                        add(t, k, c)
                        if before:
                            result(t - 1, (k - 1) % UN, c)
                        if after:
                            n = (k + 1) % UN
                            at = i * (UN // YW // 2) + (k + 1) // YW // 2
                            normalise(t + 1, n, c, loaded[n // YW % 2].done(at))
                for c in range(2):
                    normalise(0, 0, c, loaded[0].done(0))
                for k in range(UN):
                    body(0, k, k > 0, True)
                with v.Fori(1, ROUNDS - 1) as i:
                    for k in range(UN):
                        body(i, k, True, True)
                for k in range(UN):
                    body(ROUNDS - 1, k, True, k + 1 < UN)
                for c in range(2):
                    result(W - 1, UN - 1, c)

            @block.tensor
            def _(pe):
                def convolve(t, c):
                    pe.wait_ge(u_ready[c].sem, u_ready[c].done(t))
                    for d in range(3):
                        last = nc.tensor.matmul(pc[c][:], cw[:, d, :], u[c][:, :, d:d + H2], start=(d == 0), stop=(d == 2))
                    last.then_inc(conv[c].sem, 1)

                def turn(t, k, c):
                    pe.wait_ge(o_ready[c].sem, o_ready[c].done(t))
                    pe.wait_ge(fetched[c].sem, fetched[c].done(t - 2))
                    for b in range(BH):
                        last = nc.tensor.transpose(po[k % 2][c][:, b, :], o[k % 2][:, c * BH + b, :], ident[:])
                    last.then_inc(turned[c].sem, 1)

                def body(t, k, before):
                    for c in range(2):
                        convolve(t, c)
                        if before:
                            turn(t - 2, k, c)
                pe.wait_ge(const, 48)
                for k in range(UN):
                    body(k, k, k > 1)
                with pe.Fori(1, ROUNDS) as i:
                    for k in range(UN):
                        body(i * UN + k, k, True)
                for t in (W, W + 1):
                    for c in range(2):
                        turn(t - 2, t, c)

            @block.scalar
            def _(a):
                def rectify(t, k, c):
                    half = slice(c * BH, (c + 1) * BH)
                    a.wait_ge(conv[c].sem, conv[c].done(t))
                    a.wait_ge(o_ready[c].sem, o_ready[c].done(t - 2))
                    nc.scalar.activation(g[k % 2][:, half], pc[c][:], ACT.Relu, bias=cb[:, 0:1]).then_inc(relu[c].sem, 1)

                def fetch(i, k, c):
                    t = i * UN + k
                    a.wait_ge(turned[c].sem, turned[c].done(t))
                    block_, w = k // 8, 7 - k % 8
                    if k % 8 == 0 and c == 0:
                        a.wait_ge(stored[block_].sem, stored[block_].done(i - 1))
                    nc.scalar.copy(outb[block_][:, 2 * c * BH:2 * (c + 1) * BH, w, :],
                                   po[k % 2][c][:].rearrange("p b (r c) -> p (b r) c", r=2)).then_inc(
                        fetched[c].sem, 1)
                    if k % 8 == 7 and c == 1:
                        a.wait_ge(fetched[0].sem, fetched[0].done(t))
                        a.wait_ge(fetched[1].sem, fetched[1].done(t))
                        w0 = W - 8 - 8 * block_ - i * UN
                        for b in range(B):
                            a.dma_start(out[b].rearrange("(h r) w c -> h r w c", r=2)[:, :, bass.ds(w0, 8), :],
                                        outb[block_][:, 2 * b:2 * b + 2]).then_inc(stored[block_].sem, 16)

                def body(i, k, before):
                    for c in range(2):
                        rectify(i * UN + k, k, c)
                        if before:
                            fetch(*((i, k - 2) if k >= 2 else (i - 1, k + UN - 2)), c)

                a.wait_ge(const, 48)
                for k in range(UN):
                    body(0, k, k > 1)
                with a.Fori(1, ROUNDS) as i:
                    for k in range(UN):
                        body(i, k, True)
                for k in (UN - 2, UN - 1):
                    for c in range(2):
                        fetch(ROUNDS - 1, k, c)
                for s in stored:
                    a.wait_ge(s.sem, s.done(ROUNDS - 1))


WIN, HEADS, HC = 8, 4, 8


def local_mixer(nc, x, cat, ident_d, wq_d, wk_d, wv_d, bq_d, bk_d, bv_d, pos_d, mask_d, onehot_d, mean0, rstd0):
    B = x.shape[0]
    NT = B * H // (2 * WIN)
    SLABS = H // (2 * WIN)
    with Stage(nc, "attn") as p:
        xt = [p.sbuf(f"xt{i}", [P, 2, 2, WIN, C]) for i in range(2)]
        xr = p.sbuf("xr", [P, WIN, P])
        xn = p.sbuf("xn", [P, 16, 64])
        kst = [p.sbuf(f"kst{i}", [P, 8, 64]) for i in range(2)]
        qb = [[p.sbuf(f"qb{t}{s}", [P, 16, P]) for s in range(2)] for t in range(2)]
        kb = [[p.sbuf(f"kb{t}{s}", [P, 16, HEADS, 64]) for s in range(2)] for t in range(2)]
        vb = [p.sbuf(f"vb{t}", [P, 16, 2, 8, HC + 1]) for t in range(2)]
        ident, wq, wk, wv = (p.sbuf(k, [P, P]) for k in ("ident", "wq", "wk", "wv"))
        bq, bk = (p.sbuf(k, [P, 1]) for k in ("bq", "bk"))
        bqs = p.sbuf("bqs", [P, 1])
        bv = p.sbuf("bv", [P, 2, 8, HC])
        mask = p.sbuf("mask", [P, HEADS])
        row = p.sbuf("row", [1, 2, B, P])
        one = p.sbuf("one", [1, 1])
        affine = p.sbuf("affine", [P, 2, B])
        mx = [p.sbuf(f"mx{i}", [P, 16]) for i in range(2)]
        ss = [p.sbuf(f"ss{i}", [P, 16, 64]) for i in range(4)]
        pts = [p.sbuf(f"pts{i}", [P, 8, P]) for i in range(2)]
        rz = p.sbuf("rz", [P, 16])
        lo = [p.sbuf(f"lo{i}", [P, 32, 32]) for i in range(2)]
        ps = [p.psum(f"scores{i}", [P, 4, 256]) for i in range(2)]
        pt = p.psum("turned", [P, 8, P])
        po = p.psum("outputs", [P, 16, 2, HC + 1])
        pb = p.psum("prepare", [P, 512])
        const, init, passed_sp, row_ready, spread, passed_q, passed_a = (
            p.sem(k) for k in ("const", "init", "passed_sp", "row_ready", "spread", "passed_q", "passed_a"))
        x_loaded = [Event(p.sem(f"x_loaded{i}"), 16 * 2) for i in range(2)]
        stored = [[Event(p.sem(f"stored{i}{s}"), 16 * 2 * WIN) for s in range(2)] for i in range(2)]
        xr_ready, turned, xn_ready, k_made, k_staged, k_ready, q_made, q_ready, v_made, v_ready = (
            Event(p.sem(k)) for k in ("xr_ready", "x_turned", "xn_ready", "k_made", "k_staged", "k_ready", "q_made",
                                      "q_ready", "v_made", "v_ready"))
        scored, max_ready, less_ready, exp_ready, p_turned, p_a, p_v, o_made, sum_ready, o_ready = (
            Event(p.sem(k)) for k in ("scored", "max_ready", "less_ready", "exp_ready", "p_turned", "p_a", "p_v", "o_made",
                                      "sum_ready", "o_ready"))
        seed(nc, x_loaded + stored[0] + stored[1] + [xr_ready, turned, xn_ready, k_made, k_staged, k_ready, q_made, q_ready, v_made,
                                      v_ready, scored, max_ready, less_ready, exp_ready, p_turned, p_a, p_v, o_made,
                                      sum_ready, o_ready])

        def nxt(m, k):
            return (m, 1) if k == 0 else (m + 1, 0)

        def ahead(m, k, c, by):
            if c + by < 0:
                m, k = (m, 0) if k == 1 else (m - 1, 1)
            elif c + by >= 8:
                m, k = nxt(m, k)
            return m, k, (c + by) % 8

        def tiles(engine, body):
            for k in range(2):
                body(0, k, True, True)
            with engine.Fori(1, NT // 2 - 1) as m:
                for k in range(2):
                    body(m, k, True, True)
            body(NT // 2 - 1, 0, True, False)
            body(NT // 2 - 1, 1, False, False)

        def first_later(m, k):
            return not (isinstance(m, int) and m == 0 and k == 0)

        CONSTS = 9 + 2 * 2 * (16 + 16)
        with nc.Block() as block:
            @block.sync
            def _(sp):
                for t, d in ((ident, ident_d), (wq, wq_d), (wk, wk_d), (wv, wv_d), (bq, bq_d), (bk, bk_d), (bv, bv_d),
                             (mask, mask_d), (one, ident_d[0:1, 0:1])):
                    sp.dma_start(t[:], d).then_inc(const, 16)
                for t in range(2):
                    for s in range(2):
                        fixed = slice(64, 128) if s == 0 else slice(0, 64)
                        for w in range(16):
                            sp.dma_start(qb[t][s][fixed, w], onehot_d).then_inc(const, 16)
                            sp.dma_start(kb[t][s][fixed, w], pos_d).then_inc(const, 16)

                def load(m, k):
                    T = m * 2 + k
                    sp.wait_ge(xr_ready.sem, xr_ready.done(T - 2))
                    sp.sem_inc(passed_sp, 1)
                    for s in range(2):
                        rows = x[bass.ds(T // SLABS, 1), bass.ds((T % SLABS) * 16 + s * 8, 8)] if not isinstance(T, int) else \
                            x[T // SLABS:T // SLABS + 1, (T % SLABS) * 16 + s * 8:(T % SLABS) * 16 + s * 8 + 8]
                        sp.dma_start(xt[k][:, s].rearrange("p a v c -> p (a v c)"),
                                     rows.rearrange("a h (q v) c -> (a h) q (v c)", q=16)).then_inc(x_loaded[k].sem, 16)

                def store(m, k):
                    T = m * 2 + k
                    sp.wait_ge(o_ready.sem, o_ready.done(T * 8 + 7))
                    sp.sem_inc(passed_sp, 1)
                    for s in range(2):
                        rows = cat[bass.ds(T // SLABS, 1), bass.ds((T % SLABS) * 16 + s * 8, 8), :, 0:HALF] if not isinstance(T, int) \
                            else cat[T // SLABS:T // SLABS + 1, (T % SLABS) * 16 + s * 8:(T % SLABS) * 16 + s * 8 + 8, :, 0:HALF]
                        for a_ in range(2):
                            dst = rows.rearrange("a h (q w v) c -> w (a h) v q c", q=16, w=2)[a_]
                            for h in range(WIN):
                                r = 64 * a_ + WIN * h
                                sp.dma_start(dst[h], lo[k][r:r + WIN, 16 * s:16 * s + 16]).then_inc(stored[k][s].sem, 16)

                def body(m, k, n1, n2):
                    if n2:
                        load(m + 1, k)
                    store(m, k)
                load(0, 0)
                load(0, 1)
                tiles(sp, body)
                for k in range(2):
                    for s in range(2):
                        sp.wait_ge(stored[k][s].sem, stored[k][s].done(NT // 2 - 1))

            @block.gpsimd
            def _(q):
                def copy(m, k):
                    T = m * 2 + k
                    q.wait_ge(x_loaded[k].sem, x_loaded[k].done(m))
                    q.wait_ge(turned.sem, turned.done(T * 2 - 1))
                    q.wait_ge(k_ready.sem, k_ready.done((T - 1) * 2 + 1))
                    q.sem_inc(passed_q, 1)
                    for s in range(2):
                        last = nc.gpsimd.tensor_copy(
                            xr[:, :, 64 * s:64 * s + 64].rearrange("p v (a c) -> p v a c", a=2),
                            xt[k][:, s, :, :, 0:HALF].rearrange("p a v c -> p v a c"))
                    last.then_inc(xr_ready.sem, 1)

                def keys(m, k):
                    T = m * 2 + k
                    for half in range(2):
                        q.wait_ge(k_staged.sem, k_staged.done(T * 2 + half))
                        for s in range(2):
                            r = slice(64 * s, 64 * s + 64)
                            last = nc.gpsimd.tensor_tensor(
                                kb[k][s][r, 8 * half:8 * half + 8],
                                kst[half][r].unsqueeze(2).to_broadcast([64, 8, HEADS, 64]),
                                mask[r].unsqueeze(1).unsqueeze(3).to_broadcast([64, 8, HEADS, 64]), ALU.mult)
                        last.then_inc(k_ready.sem, 1)
                q.wait_ge(const, 16 * CONSTS)
                copy(0, 0)
                keys(0, 0)
                copy(0, 1)

                def body(m, k, n1, n2):
                    if n1:
                        keys(*nxt(m, k))
                    if n2:
                        copy(m + 1, k)
                tiles(q, body)

            @block.tensor
            def _(pe):
                def prepare(m, k, piece):
                    T = m * 2 + k
                    half = piece % 2
                    before = (v_ready.done(T * 2 - 1), xn_ready.done(T * 2), xn_ready.done(T * 2 + 1), k_staged.done(T * 2),
                              k_staged.done(T * 2 + 1), q_ready.done(T * 2), q_ready.done(T * 2 + 1), v_ready.done(T * 2))[piece]
                    pe.wait_ge((v_ready, xn_ready, xn_ready, k_staged, k_staged, q_ready, q_ready, v_ready)[piece].sem, before)
                    if piece < 2:
                        pe.wait_ge(xr_ready.sem, xr_ready.done(T))
                        for v_ in range(4):
                            last = nc.tensor.transpose(pb[:, 128 * v_:128 * v_ + 128], xr[:, 4 * half + v_, :], ident[:])
                        last.then_inc(turned.sem, 1)
                    elif piece < 6:
                        last = nc.tensor.matmul(pb[:], (wk if piece < 4 else wq)[:],
                                                xn[:, 8 * half:8 * half + 8].rearrange("p q t -> p (q t)"), start=True, stop=True)
                        last.then_inc((k_made if piece < 4 else q_made).sem, 1)
                    else:
                        for j in range(4):
                            w = 8 * half + 2 * j
                            last = nc.tensor.matmul(pb[:, 128 * j:128 * j + 128], xn[:, w:w + 2].rearrange("p q t -> p (q t)"),
                                                    wv[:], start=True, stop=True)
                        last.then_inc(v_made.sem, 1)

                def scores(m, k, c):
                    g, T = (m * 2 + k) * 8 + c, m * 2 + k
                    s, w0 = c // 4, 4 * (c % 4)
                    if c == 0:
                        pe.wait_ge(k_ready.sem, k_ready.done(T * 2 + 1))
                        pe.wait_ge(q_ready.sem, q_ready.done(T * 2 + 1))
                    pe.wait_ge(less_ready.sem, less_ready.done(g - 2))
                    for w in range(4):
                        last = nc.tensor.matmul(ps[c % 2][:, w], qb[k][s][:, w0 + w],
                                                kb[k][s][:, w0 + w].rearrange("p h t -> p (h t)"), start=True, stop=True)
                    last.then_inc(scored.sem, 1)

                def turn(m, k, c):
                    g = (m * 2 + k) * 8 + c
                    pe.wait_ge(exp_ready.sem, exp_ready.done(g))
                    pe.wait_ge(p_a.sem, p_a.done(g - 1))
                    pe.wait_ge(p_v.sem, p_v.done(g - 1))
                    e = ss[c % 4][:].rearrange("p (w h) t -> p w (h t)", w=8)
                    for w in range(8):
                        last = nc.tensor.transpose(pt[:, w, :], e[:, w, :], ident[:])
                    last.then_inc(p_turned.sem, 1)

                def outputs(m, k, c):
                    g, T = (m * 2 + k) * 8 + c, m * 2 + k
                    s, w0 = c // 4, 4 * (c % 4)
                    pe.wait_ge(p_a.sem, p_a.done(g))
                    pe.wait_ge(p_v.sem, p_v.done(g))
                    pe.wait_ge(v_ready.sem, v_ready.done(T * 2 + 1))
                    pe.wait_ge(o_ready.sem, o_ready.done(g - 1))
                    for w in range(4):
                        for hp in range(2):
                            v_ = vb[k][:, w0 + w].rearrange("p e (s a h) c -> p e s a h c", s=2, a=2)[:, :, s, :, hp]
                            e0 = 4 * w + 2 * hp
                            last = nc.tensor.matmul(po[:, e0:e0 + 2], pts[c % 2][:, 2 * w + hp], v_, start=True, stop=True)
                    last.then_inc(o_made.sem, 1)

                pe.wait_ge(const, 16 * CONSTS)
                pe.wait_ge(row_ready, 2)
                for a_ in range(2):
                    for b in range(B):
                        last = nc.tensor.matmul(po[:].rearrange("p e a c -> p (e a c)")[:, a_ * B + b:a_ * B + b + 1],
                                                row[0:1, a_, b, :], one[:], start=True, stop=True)
                last.then_inc(spread, 1)
                pe.wait_ge(init, 1)
                for piece in range(8):
                    prepare(0, 0, piece)
                scores(0, 0, 0)
                scores(0, 0, 1)

                def body(m, k, n1, n2):
                    for c in range(8):
                        if c < 6 or n1:
                            scores(*ahead(m, k, c, 2))
                        turn(m, k, c)
                        if n1:
                            prepare(*nxt(m, k), c)
                        if c > 0 or first_later(m, k):
                            outputs(*ahead(m, k, c, -1))
                tiles(pe, body)
                outputs(NT // 2 - 1, 1, 7)

            @block.scalar
            def _(a):
                def prepare(m, k, piece):
                    T = m * 2 + k
                    half = piece % 2
                    b = T // SLABS
                    if piece < 2:
                        a.wait_ge(turned.sem, turned.done(T * 2 + half))
                        if half == 0:
                            a.wait_ge(v_made.sem, v_made.done(T * 2 - 1))
                        a.sem_inc(passed_a, 1)
                        sc, bi = (affine[:, j, b:b + 1] if isinstance(b, int) else affine[:, j, bass.ds(b, 1)] for j in range(2))
                        for v_ in range(4):
                            last = nc.scalar.activation(
                                xn[:].rearrange("p q (h v) -> p h q v", v=WIN)[:, :, :, 4 * half + v_],
                                pb[:, 128 * v_:128 * v_ + 128].rearrange("p (h q) -> p h q", h=WIN), ACT.Identity, bias=bi, scale=sc)
                        last.then_inc(xn_ready.sem, 1)
                    elif piece < 4:
                        a.wait_ge(k_made.sem, k_made.done(T * 2 + half))
                        a.wait_ge(k_ready.sem, k_ready.done(T * 2 - 2 + half))
                        nc.scalar.activation(kst[half][:].rearrange("p q t -> p (q t)"), pb[:], ACT.Identity,
                                             bias=bk[:, 0:1]).then_inc(k_staged.sem, 1)
                    elif piece < 6:
                        a.wait_ge(q_made.sem, q_made.done(T * 2 + half))
                        for s in range(2):
                            for w in range(2):
                                r = slice(64 * s + 32 * w, 64 * s + 32 * w + 32)
                                last = nc.scalar.activation(qb[k][s][r, 8 * half:8 * half + 8, 64 * w:64 * w + 64],
                                                            pb[r].rearrange("p (q t) -> p q t", q=8), ACT.Identity,
                                                            bias=bqs[r, 0:1], scale=HC ** -0.5)
                        last.then_inc(q_ready.sem, 1)

                def exponentials(m, k, c):
                    g = (m * 2 + k) * 8 + c
                    a.wait_ge(less_ready.sem, less_ready.done(g))
                    nc.scalar.activation(ss[c % 4][:], ss[c % 4][:], ACT.Exp).then_inc(exp_ready.sem, 1)

                def fetch(m, k, c):
                    g = (m * 2 + k) * 8 + c
                    a.wait_ge(p_turned.sem, p_turned.done(g))
                    a.wait_ge(o_made.sem, o_made.done(g - 2))
                    nc.scalar.copy(pts[c % 2][:, 0:4], pt[:, 0:4]).then_inc(p_a.sem, 1)

                a.wait_ge(const, 16 * CONSTS)
                a.wait_ge(init, 1)
                for piece in range(8):
                    prepare(0, 0, piece)
                exponentials(0, 0, 0)

                def body(m, k, n1, n2):
                    for c in range(8):
                        if c < 7 or n1:
                            exponentials(*ahead(m, k, c, 1))
                        fetch(m, k, c)
                        if n1:
                            prepare(*nxt(m, k), c)
                tiles(a, body)

            @block.vector
            def _(v):
                def values(m, k, half):
                    T = m * 2 + k
                    v.wait_ge(v_made.sem, v_made.done(T * 2 + half))
                    for odd in range(2):
                        src = slice(64 * odd, 64 * odd + 64)
                        for hh in range(2):
                            dst = slice(64 * hh, 64 * hh + 64)
                            last = nc.vector.tensor_tensor(
                                vb[k][dst, 8 * half + odd:8 * half + 8:2, hh, :, 0:HC],
                                pb[src].rearrange("p (j e s c) -> p j e s c", j=4, e=2, c=HC)[:, :, hh],
                                bv[src, hh].unsqueeze(1).to_broadcast([64, 4, 8, HC]), ALU.add)
                    last.then_inc(v_ready.sem, 1)

                def maxima(m, k, c):
                    g = (m * 2 + k) * 8 + c
                    s_ = ps[c % 2][:].rearrange("p w (h t) -> p (w h) t", t=64)
                    v.wait_ge(scored.sem, scored.done(g))
                    nc.vector.tensor_reduce(mx[c % 2][:], s_, AX.X, ALU.max).then_inc(max_ready.sem, 1)
                    v.wait_ge(max_ready.sem, max_ready.done(g))
                    v.wait_ge(p_turned.sem, p_turned.done(g - 2))
                    nc.vector.tensor_tensor(ss[c % 4][:], s_, mx[c % 2][:].unsqueeze(2).to_broadcast([P, 16, 64]),
                                            ALU.subtract).then_inc(less_ready.sem, 1)

                def fetch(m, k, c):
                    g = (m * 2 + k) * 8 + c
                    v.wait_ge(p_turned.sem, p_turned.done(g))
                    v.wait_ge(o_made.sem, o_made.done(g - 2))
                    nc.vector.tensor_copy(pts[c % 2][:, 4:8], pt[:, 4:8]).then_inc(p_v.sem, 1)

                def normalise(m, k, c):
                    g = (m * 2 + k) * 8 + c
                    v.wait_ge(o_made.sem, o_made.done(g))
                    if c % 4 == 0:
                        v.wait_ge(stored[k][c // 4].sem, stored[k][c // 4].done(m - 1))
                    v.wait_ge(o_ready.sem, o_ready.done(g - 1))
                    for w in range(2):
                        r = slice(64 * w, 64 * w + 64)
                        last = nc.vector.reciprocal(rz[r], po[r, :, w, HC])
                    last.then_inc(sum_ready.sem, 1)
                    v.wait_ge(sum_ready.sem, sum_ready.done(g))
                    for w in range(2):
                        r = slice(64 * w, 64 * w + 64)
                        last = nc.vector.tensor_tensor(
                            lo[k][r, 4 * c:4 * c + 4].rearrange("p q (h c) -> p (q h) c", c=HC), po[r, :, w, 0:HC],
                            rz[r].unsqueeze(2).to_broadcast([64, 16, HC]), ALU.mult)
                    last.then_inc(o_ready.sem, 1)

                v.wait_ge(const, 16 * CONSTS)
                ng = HALF // 2
                mr = mean0.rearrange("p (b g) -> p b g", b=B)[0:1, :, 0:ng]
                rr = rstd0.rearrange("p (b g) -> p b g", b=B)[0:1, :, 0:ng]
                out_ = lambda a_, b: row[0:1, a_, b].rearrange("p (s g e) -> p s g e", s=4, e=2)
                wide = lambda t, b: t[:, b:b + 1].unsqueeze(3).to_broadcast([1, 4, ng, 2])
                for b in range(B):
                    last = nc.vector.tensor_copy(out_(0, b), wide(rr, b))
                    last = nc.vector.tensor_copy(out_(1, b), wide(mr, b))
                last.then_inc(row_ready, 1)
                v.wait_ge(row_ready, 1)
                nc.vector.scalar_tensor_tensor(out=row[0:1, 1].rearrange("p b c -> p (b c)"), in0=row[0:1, 1].rearrange("p b c -> p (b c)"),
                                               scalar=-1.0, in1=row[0:1, 0].rearrange("p b c -> p (b c)"),
                                               op0=ALU.mult, op1=ALU.mult).then_inc(row_ready, 1)
                for t in range(2):
                    for s in range(2):
                        for w in range(2):
                            r = slice(64 * s + 32 * w, 64 * s + 32 * w + 32)
                            nc.vector.memset(qb[t][s][r, :, 64 * (1 - w):64 * (1 - w) + 64], 0.0)
                    for hh in range(2):
                        r = slice(64 * hh, 64 * hh + 64)
                        nc.vector.memset(vb[t][r, :, 1 - hh], 0.0)
                        nc.vector.memset(vb[t][r, :, hh, :, HC:HC + 1], 1.0)
                nc.vector.tensor_scalar(bqs[:], bq[:], HC ** -0.5, None, ALU.mult)
                v.wait_ge(spread, 1)
                nc.vector.tensor_copy(affine[:].rearrange("p a b -> p (a b)"),
                                      po[:].rearrange("p e a c -> p (e a c)")[:, 0:2 * B]).then_inc(init, 1)
                for half in range(2):
                    values(0, 0, half)
                maxima(0, 0, 0)
                maxima(0, 0, 1)

                def body(m, k, n1, n2):
                    for c in range(8):
                        if c > 1 or first_later(m, k):
                            normalise(*ahead(m, k, c, -2))
                        if c < 6 or n1:
                            maxima(*ahead(m, k, c, 2))
                        fetch(m, k, c)
                        if n1 and c >= 6:
                            values(*nxt(m, k), c - 6)
                tiles(v, body)
                for c in (6, 7):
                    normalise(NT // 2 - 1, 1, c)


KH = H // 2 + 1
NI = 4
MAGIC = 1.5 * 2 ** 23
TWO_PI = 6.2831850


def global_mixer(nc, x, cat, dft, params, mean0, rstd0):
    B = x.shape[0]
    NG = B * HALF // NI
    GB = HALF // NI
    LAG = 3
    with Stage(nc, "mix") as p:
        xs = p.sbuf("images", [P, 2, 2, W, HALF])
        consts = {k: p.sbuf(k, list(v.shape)) for k, v in dft.items()}
        par = {k: p.sbuf(k, list(v.shape)) for k, v in params.items()}
        cospb = p.sbuf("cospb", [P, HALF])
        folded = [p.sbuf(f"folded{i}", [P, 2, W]) for i in range(2)]
        half1 = p.sbuf("half1", [P, 257])
        rows = [p.sbuf(f"rows{i}", [P, 2, 2 * KH]) for i in range(2)]
        re = [p.sbuf(f"re{i}", [P, NI, 2, KH]) for i in range(3)]
        im = [p.sbuf(f"im{i}", [P, NI, 2, KH]) for i in range(3)]
        b0, b1, b2, b3, b4, b5 = (p.sbuf(f"work{k}", [P, NI, 2, KH]) for k in range(6))
        weight, weight2 = (p.sbuf(k, [P, HALF]) for k in ("weight", "weight2"))
        half3 = p.sbuf("half3", [P, 2, 128])
        cols = [p.sbuf(f"cols{i}", [P, 2, W]) for i in range(2)]
        quarter = p.sbuf("quarter", [P, 2])
        p1 = p.psum("p1", [P, 2, 512])
        p2 = p.psum("p2", [P, 2, 512])
        p3 = [p.psum(f"p3{i}", [P, 2, 256]) for i in range(2)]
        p4 = [p.psum(f"p4{i}", [P, 2, W]) for i in range(2)]
        const, init, passed_sp, passed_q, passed_a = (p.sem(k) for k in ("const", "init", "passed_sp", "passed_q", "passed_a"))
        x_loaded, x_stored = (Event(p.sem(k), 32) for k in ("x_loaded", "x_stored"))
        fold_ready, rows_made, half1_ready, rows_ready, spec_made, spec_ready = (
            Event(p.sem(k)) for k in ("fold_ready", "rows_made", "half1_ready", "rows_ready", "spec_made", "spec_ready"))
        cols_made, half3_ready, cols_ready, image_made, image_ready = (
            Event(p.sem(k)) for k in ("cols_made", "half3_ready", "cols_ready", "image_made", "image_ready"))
        ACT_STEPS, TRIG_STEPS, DVE_STEPS, POOL_STEPS, OFFSET_STEPS = 3, 3, 21, 11, 2
        cols_made.seed = 16
        act_step, dve_step, pool_step = (Event(p.sem(k), seed=60) for k in ("act_step", "dve_step", "pool_step"))
        offset_step, trig_step = Event(p.sem("offset_step")), Event(p.sem("trig_step"))
        seed(nc, [offset_step, trig_step, x_loaded, x_stored, fold_ready, rows_made, half1_ready, rows_ready, spec_made, spec_ready, cols_made,
                  half3_ready, cols_ready, image_made, image_ready, act_step, dve_step, pool_step])
        flat = lambda t: t[:].rearrange("p a b c -> p (a b c)")

        def columns(t, at, size=1):
            return t[:, at:at + size] if isinstance(at, int) else t[:, bass.ds(at, size)]

        def pipeline(engine, slot):
            def body(n, fwd, point, last, back, at):
                for j in range(NI):
                    slot(n, j, fwd, point, last, last if j >= LAG else back, back, at)
            body(-1, True, False, False, False, 2)
            body(0, True, True, False, False, 0)
            body(1, True, True, True, False, 1)
            rounds = (NG - 3) // 3
            with engine.Fori(0, rounds) as i:
                for k in range(3):
                    body(i * 3 + (2 + k), True, True, True, True, (2 + k) % 3)
            for n in range(2 + 3 * rounds, NG - 1):
                body(n, True, True, True, True, n % 3)
            body(NG - 1, False, True, True, True, (NG - 1) % 3)
            body(NG, False, False, True, True, NG % 3)
            body(NG + 1, False, False, False, True, (NG + 1) % 3)

        with nc.Block() as block:
            @block.sync
            def _(sp):
                for k in consts:
                    sp.dma_start(consts[k][:], dft[k]).then_inc(const, 16)
                for k in par:
                    sp.dma_start(par[k][:], params[k]).then_inc(const, 16)

                def load(b, buf):
                    for hh in range(2):
                        sp.dma_start(xs[:, bass.ds(buf, 1), hh].rearrange("p a w c -> p (a w) c"),
                                     x[bass.ds(b, 1), hh * P:(hh + 1) * P, :, HALF:C].rearrange("a p w c -> (a p) w c")
                                     ).then_inc(x_loaded.sem, 16)

                def store(b, buf):
                    sp.wait_ge(image_ready.sem, image_ready.done(b * HALF + HALF - 1))
                    sp.sem_inc(passed_sp, 1)
                    for hh in range(2):
                        sp.dma_start(cat[bass.ds(b, 1), hh * P:(hh + 1) * P, :, HALF:C].rearrange("a p w c -> (a p) w c"),
                                     xs[:, bass.ds(buf, 1), hh].rearrange("p a w c -> p (a w) c")).then_inc(x_stored.sem, 16)
                load(0, 0)
                with sp.Fori(0, B - 1) as b:
                    sp.wait_ge(x_loaded.sem, x_loaded.done(b))
                    sp.wait_ge(x_stored.sem, x_stored.done(b - 1))
                    sp.sem_inc(passed_sp, 1)
                    load(b + 1, (b + 1) % 2)
                    store(b, b % 2)
                store(B - 1, (B - 1) % 2)
                sp.wait_ge(x_stored.sem, x_stored.done(B - 1))

            @block.tensor
            def _(pe):
                pe.wait_ge(const, 16 * (len(consts) + len(par)))

                def row_product(t, j):
                    f = folded[j % 2]
                    pe.wait_ge(fold_ready.sem, fold_ready.done(t))
                    pe.wait_ge(rows_ready.sem, rows_ready.done(t - 1))
                    for wh in range(2):
                        e, o = f[:, 0, wh * P:(wh + 1) * P], f[:, 1, wh * P:(wh + 1) * P]
                        nc.tensor.matmul(p1[:, wh, 0:256].rearrange("p (s k) -> p s k", s=2)[:, :, 0:65], e,
                                         consts["rows_even"][:].rearrange("p (s k) -> p s k", s=2), start=True, stop=True)
                        last = nc.tensor.matmul(p1[:, wh, 64:322].rearrange("p (s k) -> p s k", s=2)[:, :, 0:64], o,
                                                consts["rows_odd"][:].rearrange("p (s k) -> p s k", s=2), start=True, stop=True)
                    last.then_inc(rows_made.sem, 1)

                def column_product(t, j):
                    r = rows[j % 2]
                    pe.wait_ge(rows_ready.sem, rows_ready.done(t))
                    pe.wait_ge(spec_ready.sem, spec_ready.done(t - 1))
                    for q in range(2):
                        c, s, ms = (consts["columns"][:, 3 * q + k, :] for k in range(3))
                        nc.tensor.matmul(p2[:, q, 0:2 * KH], c, r[:, q, :], start=True, stop=False)
                        nc.tensor.matmul(p2[:, q, 0:KH], s, r[:, q, KH:2 * KH], start=False, stop=False)
                        last = nc.tensor.matmul(p2[:, q, KH:2 * KH], ms, r[:, q, 0:KH], start=False, stop=True)
                    last.then_inc(spec_made.sem, 1)

                def column_product_back(u, j, at):
                    pe.wait_ge(cols_ready.sem, cols_ready.done(u - 2))
                    for q in range(2):
                        c, s, ms = ((consts["columns"] if q == 0 else consts["columns_back"])[:, k, :] for k in range(3))
                        a_, b_ = re[at][:, j, q, :], im[at][:, j, q, :]
                        nc.tensor.matmul(p3[j % 2][:, q, 0:128], a_[:, 1:KH], c, start=True, stop=False)
                        nc.tensor.matmul(p3[j % 2][:, q, 0:128], b_[:, 1:KH], ms, start=False, stop=True)
                        nc.tensor.matmul(p3[j % 2][:, q, 128:256], a_[:, 0:128], s, start=True, stop=False)
                        last = nc.tensor.matmul(p3[j % 2][:, q, 128:256], b_[:, 0:128], c, start=False, stop=True)
                    last.then_inc(cols_made.sem, 1)

                def row_product_back(u, j):
                    pe.wait_ge(cols_ready.sem, cols_ready.done(u))
                    pe.wait_ge(image_ready.sem, image_ready.done(u - 2))
                    for hh in range(2):
                        nc.tensor.matmul(p4[j % 2][:, hh, :], consts["rows_back"][:, 0, hh * P:(hh + 1) * P], cols[j % 2][:, 0, :],
                                         start=True, stop=False)
                        last = nc.tensor.matmul(p4[j % 2][:, hh, :], consts["rows_back"][:, 1, hh * P:(hh + 1) * P],
                                                cols[j % 2][:, 1, :], start=False, stop=True)
                    last.then_inc(image_made.sem, 1)

                def slot(n, j, fwd, point, last, inv, back, at):
                    t, u, ju = (n + 1) * NI + j, (n - 1) * NI + j - LAG, (j - LAG) % NI
                    if fwd:
                        row_product(t, j)
                    if back:
                        row_product_back((n - 2) * NI + j, j)
                    if inv:
                        if j == LAG:
                            pe.wait_ge(offset_step.sem, offset_step.done(n * OFFSET_STEPS - 1))
                        column_product_back(u, ju, (at - (1 if j >= LAG else 2)) % 3)
                    if fwd:
                        column_product(t, j)
                pipeline(pe, slot)

            @block.scalar
            def _(a):
                a.wait_ge(const, 16 * (len(consts) + len(par)))
                a.wait_ge(init, 4)
                nc.scalar.activation(cospb[:], cospb[:], ACT.Sin, scale=-TWO_PI, bias=quarter[:, 0:1]).then_inc(init, 1)

                def step(n, k, ins):
                    ins.then_inc(act_step.sem, 1)

                def slot(n, j, fwd, point, last, inv, back, at):
                    RE, IM = flat(re[at]), flat(im[at])
                    t, u, ju = (n + 1) * NI + j, (n - 1) * NI + j - LAG, (j - LAG) % NI
                    act = nc.scalar.activation
                    if fwd:
                        a.wait_ge(rows_made.sem, rows_made.done(t))
                        a.wait_ge(rows_ready.sem, rows_ready.done(t - 1))
                        nc.scalar.copy(half1[:], p1[:, 1, 0:257]).then_inc(half1_ready.sem, 1)
                    if point and j == 1:
                        a.wait_ge(pool_step.sem, pool_step.done(n * POOL_STEPS + 2))
                        step(n, 0, act(flat(b3), flat(b3), ACT.Sqrt, bias=quarter[:, 1:2]))
                        a.wait_ge(trig_step.sem, trig_step.done((n - 1) * TRIG_STEPS + 1))
                        step(n, 1, act(flat(b0), RE, ACT.Abs))
                    if back:
                        a.wait_ge(image_made.sem, image_made.done((n - 2) * NI + j))
                        a.sem_inc(passed_a, 1)
                        nc.scalar.activation(image_out(n - 2, j), p4[j % 2][:], ACT.Abs).then_inc(image_ready.sem, 1)
                    if inv:
                        a.wait_ge(cols_made.sem, cols_made.done(u))
                        a.wait_ge(cols_ready.sem, cols_ready.done(u - 1))
                        nc.scalar.copy(half3[:].rearrange("p a b -> p (a b)"), p3[ju % 2][:, 1, :]).then_inc(half3_ready.sem, 1)
                    if last and j == 0:
                        a.wait_ge(dve_step.sem, dve_step.done((n - 1) * DVE_STEPS + 18))
                        trig(n - 1, 0, act(flat(b0), flat(b1), ACT.Abs))
                        a.wait_ge(trig_step.sem, trig_step.done((n - 1) * TRIG_STEPS + 0))
                        trig(n - 1, 1, act(flat(b5), flat(b0), ACT.Sin, scale=-TWO_PI, bias=quarter[:, 0:1]))
                        trig(n - 1, 2, act(flat(b1), flat(b1), ACT.Sin, scale=TWO_PI))
                    if point and j == 3:
                        a.wait_ge(pool_step.sem, pool_step.done(n * POOL_STEPS + 7))
                        step(n, 2, act(flat(b3), flat(b1), ACT.Arctan))
                    if fwd:
                        a.wait_ge(spec_made.sem, spec_made.done(t))
                        a.wait_ge(cols_made.sem, cols_made.done((n - 2) * NI + j))
                        nc.scalar.copy(re[(at + 1) % 3][:, j], p2[:, :, 0:KH])
                        nc.scalar.copy(im[(at + 1) % 3][:, j], p2[:, :, KH:2 * KH]).then_inc(spec_ready.sem, 1)

                def trig(n, k, ins):
                    ins.then_inc(trig_step.sem, 1)

                def image_out(n, j):
                    if isinstance(n, int):
                        return xs[:, (n // GB) % 2, :, :, (n % GB) * NI + j]
                    return xs[:, bass.ds((n // GB) % 2, 1), :, :, bass.ds((n % GB) * NI + j, 1)].rearrange(
                        "p a h w c -> p (a h) (w c)")
                pipeline(a, slot)

            @block.gpsimd
            def _(q):
                def step(n, k, ins):
                    ins.then_inc(pool_step.sem, 1)

                def own(n, k):
                    q.wait_ge(pool_step.sem, pool_step.done(n * POOL_STEPS + k))

                def slot(n, j, fwd, point, last, inv, back, at):
                    tt = nc.gpsimd.tensor_tensor
                    t = (n + 1) * NI + j
                    images = lambda t: t[:].rearrange("p n a b -> p n (a b)")
                    pair = lambda t, k: t[:, 2 * k:2 * k + 2].rearrange("p n a b -> p (n a b)")
                    if point and j == 0:
                        own(n, 1)
                        step(n, 2, tt(flat(b3), flat(b3), flat(b4), ALU.add))
                        q.wait_ge(act_step.sem, act_step.done(n * ACT_STEPS + 1))
                        step(n, 3, tt(flat(b0), flat(b0), flat(b3), ALU.add))
                    elif point and j == 1:
                        q.wait_ge(dve_step.sem, dve_step.done(n * DVE_STEPS + 0))
                        step(n, 4, tt(flat(b5), flat(b5), flat(b4), ALU.mult))
                        step(n, 5, new_amplitude(b3, "amp_w", n * NI, ALU.mult))
                    if last and j == 1:
                        for k, g_ in enumerate((re[(at - 1) % 3], im[(at - 1) % 3])):
                            q.wait_ge(dve_step.sem, dve_step.done((n - 1) * DVE_STEPS + 19 + k))
                            tt(images(g_), images(g_), consts["offset"][:, k:k + 1, :].to_broadcast([P, NI, 2 * KH]),
                               ALU.add).then_inc(offset_step.sem, 1)
                    if point and j == 2:
                        for k in range(2):
                            q.wait_ge(dve_step.sem, dve_step.done(n * DVE_STEPS + (1, 6)[k]))
                            step(n, 6 + k, tt(pair(b1, k), pair(im[at], k), pair(b0, k), ALU.mult))
                    elif point and j == 3:
                        own(n, 7)
                        q.sem_inc(passed_q, 1)
                        step(n, 8, new_amplitude(b2, "amp_b", (n % GB) * NI, ALU.add))
                        own(n, 8)
                        chs = columns(cospb, (n % GB) * NI, NI)
                        for k, row in enumerate((0, 64)):
                            step(n, 9 + k, tt(b2[row:row + 1, :, 0, 1:128], b2[row:row + 1, :, 0, 1:128],
                                              chs[row:row + 1].unsqueeze(2).to_broadcast([1, NI, 127]), ALU.mult))

                    if fwd and j == NI - 1:
                        new, squares = n + 1, (flat(re[(at + 1) % 3]), flat(im[(at + 1) % 3]))
                        own(n, 10)
                        q.wait_ge(spec_ready.sem, spec_ready.done(t))
                        q.wait_ge(dve_step.sem, dve_step.done(n * DVE_STEPS + 16))
                        for k, (to, part) in enumerate(zip((b3, b4), squares)):
                            step(new, k, tt(flat(to), part, part, ALU.mult))

                def new_amplitude(amplitude, name, column, op):
                    of = lambda t: t[:].rearrange("p n a b -> p n (a b)")
                    return nc.gpsimd.tensor_tensor(of(b2), of(amplitude), columns(par[name], column, NI).unsqueeze(2).to_broadcast(
                        [P, NI, 2 * KH]), op)
                q.wait_ge(init, 5)
                pipeline(q, slot)

            @block.vector
            def _(v):
                v.wait_ge(const, 16 * (len(consts) + len(par)))
                tt, ts, stt = nc.vector.tensor_tensor, nc.vector.tensor_scalar, nc.vector.scalar_tensor_tensor
                nc.vector.memset(quarter[:, 0:1], float(np.pi / 2)).then_inc(init, 1)
                nc.vector.memset(quarter[:, 1:2], 1e-30)
                ts(weight[:], par["pha_w"][:], float(1 / np.pi), None, ALU.mult)
                ts(weight2[:], par["pha_w"][:], float(-2 / np.pi), None, ALU.mult)
                nc.vector.memset(rows[0][:], 0.0)
                nc.vector.memset(rows[1][:], 0.0)
                pbt = par["pha_b"]
                ts(pbt[:], pbt[:], float(1 / (2 * np.pi)), None, ALU.mult).then_inc(init, 1)
                v.wait_ge(init, 2)
                ts(cospb[:], pbt[:], MAGIC, MAGIC, ALU.add, ALU.subtract).then_inc(init, 1)
                v.wait_ge(init, 3)
                tt(cospb[:], pbt[:], cospb[:], ALU.subtract).then_inc(fold_init := p.sem("fold_init"), 1)
                v.wait_ge(fold_init, 1)
                g0 = HALF // 2
                up = lambda t: t.rearrange("p (b g) -> p b g", b=B)[:, :, g0:].unsqueeze(3).to_broadcast([P, B, g0, 2])
                aw = par["amp_w"][:].rearrange("p (b g two) -> p b g two", b=B, two=2)
                m2 = p.sbuf("mean2", [P, B * HALF])
                for b in range(B):
                    tt(aw[:, b], aw[:, b], up(rstd0)[:, b], ALU.mult)
                    ts(m2[:].rearrange("p (b g two) -> p b g two", b=B, two=2)[:, b], up(mean0)[:, b], -2.0, None, ALU.mult)
                stt(out=cospb[:], in0=cospb[:], scalar=-1.0, in1=cospb[:], op0=ALU.mult, op1=ALU.max).then_inc(init, 1)
                v.wait_ge(init, 4)
                v.drain()

                def fold_rows(n, j):
                    t = n * NI + j
                    if isinstance(n, int):
                        src = xs[:, (n // GB) % 2, :, :, (n % GB) * NI + j]
                    else:
                        src = xs[:, bass.ds((n // GB) % 2, 1), :, :, bass.ds((n % GB) * NI + j, 1)].rearrange(
                            "p a h w c -> p (a h) (w c)")
                    m = columns(m2, t)
                    v.wait_ge(x_loaded.sem, x_loaded.done(n // GB))
                    v.wait_ge(rows_made.sem, rows_made.done(t - 2))
                    stt(out=folded[j % 2][:, 0], in0=src[:, 0], scalar=m, in1=src[:, 1], op0=ALU.add, op1=ALU.add)
                    tt(folded[j % 2][:, 1], src[:, 0], src[:, 1], ALU.subtract).then_inc(fold_ready.sem, 1)

                def step(n, k, ins):
                    ins.then_inc(dve_step.sem, 1)

                def own(n, k):
                    v.wait_ge(dve_step.sem, dve_step.done(n * DVE_STEPS + k))

                def by_image(n, k, in0, scalar, in1):
                    of = lambda t_, i_: t_[:, i_].rearrange("p a b -> p (a b)") if len(t_.shape) == 4 else t_
                    for i_ in range(NI):
                        step(n, k + i_, stt(out=of(b5, i_), in0=of(in0, i_), scalar=columns(scalar, (n % GB) * NI + i_),
                                            in1=of(in1, i_), op0=ALU.mult, op1=ALU.add))

                def invert(n, k, half):
                    pair = b0[:, 2 * half:2 * half + 2].rearrange("p n a b -> p (n a b)")
                    step(n, k, nc.vector.reciprocal(pair, pair))

                def slot(n, j, fwd, point, last, inv, back, at):
                    RE, IM = flat(re[at]), flat(im[at])
                    t, u, ju = (n + 1) * NI + j, (n - 1) * NI + j - LAG, (j - LAG) % NI
                    if isinstance(n, int) and n == -1 and j == 0:
                        fold_rows(0, 0)
                    if fwd:
                        v.wait_ge(half1_ready.sem, half1_ready.done(t))
                        v.wait_ge(spec_made.sem, spec_made.done(t - 2))
                        tt(rows[j % 2][:, 0, 0:257], p1[:, 0, 0:257], half1[:], ALU.add)
                        tt(rows[j % 2][:, 1, 0:257], p1[:, 0, 0:257], half1[:], ALU.subtract).then_inc(rows_ready.sem, 1)
                    if inv:
                        v.wait_ge(half3_ready.sem, half3_ready.done(u))
                        v.wait_ge(image_made.sem, image_made.done(u - 2))
                        e = p3[ju % 2][:, 0, :].rearrange("p (s w) -> p s w", s=2)
                        tt(cols[ju % 2][:, :, 0:128], e, half3[:], ALU.add)
                        tt(cols[ju % 2][:, :, 128:256], e, half3[:], ALU.subtract).then_inc(cols_ready.sem, 1)
                    if fwd:
                        if j + 1 < NI:
                            fold_rows(n + 1, j + 1)
                        elif not (isinstance(n, int) and n + 2 >= NG):
                            fold_rows(n + 2, 0)
                    if last and j == 0:
                        v.wait_ge(pool_step.sem, pool_step.done((n - 1) * POOL_STEPS + 10))
                        v.wait_ge(trig_step.sem, trig_step.done((n - 1) * TRIG_STEPS + 1))
                        step(n - 1, 19, tt(flat(re[(at - 1) % 3]), flat(b2), flat(b5), ALU.mult))
                        v.wait_ge(trig_step.sem, trig_step.done((n - 1) * TRIG_STEPS + 2))
                        step(n - 1, 20, tt(flat(im[(at - 1) % 3]), flat(b2), flat(b1), ALU.mult))
                    if point and j == 0:
                        v.wait_ge(spec_ready.sem, spec_ready.done(n * NI + NI - 1))
                        v.wait_ge(pool_step.sem, pool_step.done(n * POOL_STEPS + 2))
                        ts(flat(b4), RE, 0.0, None, ALU.is_lt)
                        own(n - 1, 19)
                        step(n, 0, ts(flat(b5), IM, 0.0, -0.5, ALU.is_ge, ALU.add))
                    elif point and j == 1:
                        v.wait_ge(pool_step.sem, pool_step.done(n * POOL_STEPS + 3))
                        invert(n, 1, 0)
                        v.wait_ge(pool_step.sem, pool_step.done(n * POOL_STEPS + 4))
                        for i_ in range(NI):
                            one = lambda t_: t_[:, i_].rearrange("p a b -> p (a b)")
                            at_ = (n % GB) * NI + i_
                            step(n, 2 + i_, ts(one(b4), one(b4), columns(weight2, at_), columns(weight, at_), ALU.mult, ALU.add))
                    elif point and j == 2:
                        invert(n, 6, 1)
                        by_image(n, 7, b5, par["pha_w"], consts["turn"][:, 1, :])
                    elif point:
                        own(n, 10)
                        by_image(n, 11, consts["turn"][:, 0, :], pbt, b5)
                        v.wait_ge(act_step.sem, act_step.done(n * ACT_STEPS + 2))
                        step(n, 15, tt(flat(b3), flat(b3), flat(b4), ALU.mult))
                        own(n, 15)
                        step(n, 16, tt(flat(b1), flat(b3), flat(b5), ALU.add))
                        own(n, 16)
                        step(n, 17, ts(flat(b0), flat(b1), MAGIC, MAGIC, ALU.add, ALU.subtract))
                        own(n, 17)
                        step(n, 18, tt(flat(b1), flat(b1), flat(b0), ALU.subtract))
                pipeline(v, slot)


def constants():
    ch = np.arange(P)
    group1 = (ch[:, None] % C // 2 == ch[None, :] % C // 2).astype(np.float32)
    i = np.arange(P)
    rest = np.concatenate([np.arange(2, 128, 2), np.arange(1, 128, 2)])
    cos = lambda a, b: np.cos(2 * np.pi * ((a[:, None] * b[None, :]) % W) / W)
    sin = lambda a, b: np.where((a[:, None] * b[None, :]) % 128 == 0, 0.0, np.sin(2 * np.pi * ((a[:, None] * b[None, :]) % W) / W))
    even, odd = rest[:63], rest[63:]
    z = np.zeros((P, 1))
    col = lambda k: np.array([k])
    kw = [2 * i, 2 * i + 1]
    h = np.arange(H)
    side = [np.where((k == 0) | (k == 128), 0.0, np.where(k < 128, 1.0, -1.0)) for k in kw]
    turn = np.zeros((P, 2, 2, KH))
    offset = np.zeros((P, 2, 2, KH))
    for q in range(2):
        turn[:, 0, q, :] = side[q][:, None]
        turn[:, 1, q, 0] = 0.25
        offset[:, 0, q, :] = 2e-8
        offset[:, 0, q, 0] = -1e-8 * side[q]
        offset[:, 1, q, :] = 1e-8 * side[q][:, None]
        offset[:, 1, q, 0] = 2e-8
    turn[[0, 64], 0, 0, 0] = turn[[0, 64], 0, 0, KH - 1] = 1.0
    dft = {
        "rows_even": np.concatenate([cos(i, col(128)), cos(i, even), z, cos(i, col(0)), z, -sin(i, even)], 1),
        "rows_odd": np.concatenate([cos(i, odd), -sin(i, odd)], 1),
        "columns": np.stack([m for k in kw for m in (cos(i, k), sin(i, k), -sin(i, k))], 1),
        "columns_back": np.stack([cos(kw[1], i), sin(kw[1], i), -sin(kw[1], i)], 1),
        "rows_back": np.stack([np.concatenate([2 * cos(rest, h), cos(col(0), h)]),
                               np.concatenate([cos(col(128), h), -2 * sin(rest, h)])], 1) / (H * W),
        "turn": turn.reshape(P, 2, 2 * KH),
        "offset": offset.reshape(P, 2, 2 * KH),
    }
    head = (np.arange(P)[:, None] % HALF) // HC == np.arange(HEADS)[None, :]
    return {
        "mask": head.astype(np.float32),
        "onehot": np.concatenate([np.eye(64), np.eye(64)], 1).astype(np.float32),
        "dft": {k: np.ascontiguousarray(m, np.float32) for k, m in dft.items()},
        "ident": np.eye(P, dtype=np.float32),
        "avg0": np.full((P, P), 1.0 / (P * 4), np.float32),
        "avg1": group1 * np.float32(1.0 / (4 * 2 * 2 * W // 8)),
    }


def attention_layout(w_qkv, b_qkv):
    q, k, v = (w_qkv[HALF * i:HALF * i + HALF] for i in range(3))

    def diagonal(m):
        out = np.zeros((4, HALF, 4, HALF), m.dtype)
        for i in range(4):
            out[i, :, i, :] = m.T
        return out
    wv = diagonal(v).reshape(4, HALF, 4, 2, 2, HC).transpose(0, 1, 4, 2, 3, 5)
    bq, bk, bv = (b_qkv[HALF * i:HALF * i + HALF] for i in range(3))
    return (np.ascontiguousarray(diagonal(q).reshape(P, P)), np.ascontiguousarray(diagonal(k).reshape(P, P)),
            np.ascontiguousarray(wv.reshape(P, P)), np.tile(bq, 4)[:, None].copy(), np.tile(bk, 4)[:, None].copy(),
            np.ascontiguousarray(np.broadcast_to(bv.reshape(2, 2, HC).transpose(1, 0, 2)[None, :, None], (P, 2, 4, 2, HC))).reshape(P, 2, 8, HC))


def conv_layout(w):
    m = np.zeros((2, C, 3, 2, C), w.dtype)
    for d in range(3):
        for pi in range(2):
            for po in range(2):
                tap = 2 * (d - 1) + pi - po + 2
                if 0 <= tap < 5:
                    m[pi, :, d, po, :] = w[:, tap, 0, :]
    return np.ascontiguousarray(m.reshape(P, 3, P))


def build(nc, out, x, params, dft, **a):
    B = x.shape[0]
    cat = nc.dram_tensor("cat", [B, H, W, C], F32).ap()
    y = nc.dram_tensor("y", [W // YW, P, B, 2, YW, H // 4], F32).ap()
    with Stage(nc, "norm") as p:
        mean0, rstd0 = (p.sbuf(k, [P, B * GROUPS])[:] for k in ("mean0", "rstd0"))
        mean1, rstd1 = (p.sbuf(k, [P, B])[:] for k in ("mean1", "rstd1"))
        input_statistics(nc, x, a["avg0"], mean0, rstd0)
        local_mixer(nc, x, cat, a["ident"], a["wq"], a["wk"], a["wv"], a["bq"], a["bk"], a["bv"], a["pos"], a["mask"],
                    a["onehot"], mean0, rstd0)
        global_mixer(nc, x, cat, dft, params, mean0, rstd0)
        project(nc, x, cat, y, a["ident"], a["proj_w"], a["proj_b"], a["avg1"], mean1, rstd1)
        scan(nc, y, out, a["ident"], a["conv_w"], a["conv_b"], mean1, rstd1)


def kernel(x, L0_conv_w_qkv, L0_conv_b_qkv, L0_conv_pos_emb, L0_conv_amp_w, L0_conv_amp_b, L0_conv_pha_w, L0_conv_pha_b,
           L0_conv_proj_w, L0_conv_proj_b, L1_conv_w, L1_conv_b):
    import concourse.bacc as bacc
    from concourse.bass_utils import run_bass_kernel_spmd

    asarray = lambda t: np.ascontiguousarray(np.asarray(t))
    x = asarray(x)
    B = x.shape[0]
    fixed = constants()
    wq, wk, wv, bq, bk, bv = attention_layout(asarray(L0_conv_w_qkv), asarray(L0_conv_b_qkv))
    per_image = lambda t, n: np.ascontiguousarray(np.broadcast_to(np.tile(asarray(t), n), (P, n * HALF)))
    arrays = {
        "x": x, "wq": wq, "wk": wk, "wv": wv, "bq": bq, "bk": bk, "bv": bv,
        "pos": np.ascontiguousarray(asarray(L0_conv_pos_emb)[0].transpose(1, 0, 2)),
        "proj_w": np.concatenate([asarray(L0_conv_proj_w).T, np.eye(C, dtype=np.float32)]),
        "proj_b": np.ascontiguousarray(np.tile(asarray(L0_conv_proj_b), 2)[:, None]),
        "conv_w": conv_layout(asarray(L1_conv_w)),
        "conv_b": np.ascontiguousarray(np.tile(asarray(L1_conv_b), 2)[:, None]),
    }
    arrays |= {k: fixed[k] for k in ("ident", "avg0", "avg1", "mask", "onehot")}
    params = {"amp_w": per_image(L0_conv_amp_w, B), "amp_b": per_image(L0_conv_amp_b, 1),
              "pha_w": per_image(L0_conv_pha_w, 1), "pha_b": per_image(L0_conv_pha_b, 1)}
    nc = bacc.Bacc("TRN2", target_bir_lowering=False, num_devices=1)
    sent = {}

    def declare(prefix, group):
        found = {}
        for k, t in group.items():
            sent[prefix + k] = t
            found[k] = nc.dram_tensor(prefix + k, t.shape, mybir.dt.from_np(t.dtype), kind="ExternalInput").ap()
        return found
    tensors, par, dft = declare("in_", arrays), declare("par_", params), declare("dft_", fixed["dft"])
    out = nc.dram_tensor("out", x.shape, F32, kind="ExternalOutput").ap()
    build(nc, out, params=par, dft=dft, **tensors)
    return run_bass_kernel_spmd(nc, [sent], core_ids=[0]).results[0]["out"]
```
